# Optimizing a Trainium2 kernel written in Bass

```python
import numpy as np
import jax
import jax.numpy as jnp

def _softmax(x, axis=-1):
    return jax.nn.softmax(x, axis=axis)

def _gelu(x):
    return jax.nn.gelu(x, approximate=True)

def _silu(x):
    return jax.nn.silu(x)

def _sigmoid(x):
    return jax.nn.sigmoid(x)

def _layernorm(x, axis=-1, eps=1e-05):
    m = jnp.mean(x, axis=axis, keepdims=True)
    v = jnp.var(x, axis=axis, keepdims=True)
    return (x - m) / jnp.sqrt(v + eps)

def _scatter_add(tgt, idx, src, axis=0):
    return tgt.at[idx].add(src)

def _segment_sum(src, seg, n):
    return jax.ops.segment_sum(src, seg, n)
kernel_name = 'mk_gnn_ffn_d1_gnn_r8_df852d'

def setup_inputs(seed: int=0):
    np.random.seed(seed)
    _w = jnp.asarray

    def _rec_inputs():
        import jax
        import jax.numpy as jnp
        _gk = jax.random.key(seed)
        x = -0.0001884 + 1 * jax.random.normal(jax.random.fold_in(_gk, 1), (12500, 256), jnp.float32)
        _s = jax.random.randint(jax.random.fold_in(_gk, 2), (100000,), 0, 12500, jnp.int32)
        _d = jax.random.randint(jax.random.fold_in(_gk, 3), (100000,), 0, 12500, jnp.int32)
        _loop = jnp.arange(12500, dtype=jnp.int32)
        src = jnp.concatenate([_s, _d, _loop])
        dst = jnp.concatenate([_d, _s, _loop])
        _o = jnp.argsort(dst, stable=True)
        src = src[_o]
        dst = dst[_o]
        edge_weight = -0.000423496 + 0.100023 * jax.random.normal(jax.random.fold_in(_gk, 12), (212500,), jnp.float32)
        return (x, src, dst, edge_weight)
    x, src, dst, edge_weight = _rec_inputs()

    def _L0_gnn_setup():
        import jax, jax.numpy as jnp
        import numpy as np
        BLOCK_DIMS = [8] * 32

        def _mask_indices():
            d = sum(BLOCK_DIMS)
            mask = np.ones((d, d), dtype=np.int8)
            off = 0
            for b in BLOCK_DIMS:
                mask[off:off + b, off:off + b] = 0
                off += b
            rows, cols = np.nonzero(mask)
            return (d, rows.astype(np.int32), cols.astype(np.int32))
        key = jax.random.key(seed)
        k1, k2 = jax.random.split(key)
        d, rows, cols = _mask_indices()
        N = 62500
        X = jax.random.normal(k1, (N, d), dtype=jnp.float32)
        w_est = 0.1 * jax.random.normal(k2, (rows.shape[0],), dtype=jnp.float32)
        return {'X': X, 'w_est': w_est, 'rows': jnp.asarray(rows), 'cols': jnp.asarray(cols)}
    _L0_gnn_all = _L0_gnn_setup()
    _L0_gnn_in = {k: v for k, v in _L0_gnn_all.items() if k in ()}
    del _L0_gnn_all

    def _L0_ffn_setup():
        import jax, jax.numpy as jnp
        import numpy as np
        E = 8
        K = 2
        D = 256
        H = 512
        DOUT = 256
        EPS = 1e-05
        key = jax.random.key(seed)
        ks = jax.random.split(key, 9)
        s = 0.02
        return {'x': jax.random.normal(ks[0], (4, 1024, D), jnp.float32), 'gamma': 1.0 + 0.05 * jax.random.normal(ks[1], (D,), jnp.float32), 'beta': 0.05 * jax.random.normal(ks[2], (D,), jnp.float32), 'Wr': 0.01 * jax.random.normal(ks[3], (D, E), jnp.float32), 'br': jnp.zeros((E,), jnp.float32), 'W1': s * jax.random.normal(ks[4], (E, D, H), jnp.float32), 'b1': s * jax.random.normal(ks[5], (E, H), jnp.float32), 'W2': s * jax.random.normal(ks[6], (E, H, DOUT), jnp.float32), 'b2': s * jax.random.normal(ks[7], (E, DOUT), jnp.float32)}
    _L0_ffn_all = _L0_ffn_setup()
    _L0_ffn_in = {k: v for k, v in _L0_ffn_all.items() if k in ('gamma', 'beta', 'Wr', 'br', 'W1', 'b1', 'W2', 'b2')}
    del _L0_ffn_all
    return {'x': x, 'src': src, 'dst': dst, 'edge_weight': edge_weight, 'L0_ffn_gamma': _L0_ffn_in['gamma'], 'L0_ffn_beta': _L0_ffn_in['beta'], 'L0_ffn_Wr': _L0_ffn_in['Wr'], 'L0_ffn_br': _L0_ffn_in['br'], 'L0_ffn_W1': _L0_ffn_in['W1'], 'L0_ffn_b1': _L0_ffn_in['b1'], 'L0_ffn_W2': _L0_ffn_in['W2'], 'L0_ffn_b2': _L0_ffn_in['b2']}

def reference(x, src, dst, edge_weight, L0_ffn_gamma, L0_ffn_beta, L0_ffn_Wr, L0_ffn_br, L0_ffn_W1, L0_ffn_b1, L0_ffn_W2, L0_ffn_b2):
    import jax
    import jax.numpy as jnp

    def _L0_gnn_ref(X, w_est, rows, cols):
        import jax, jax.numpy as jnp
        import numpy as np
        BLOCK_DIMS = [8] * 32

        def _mask_indices():
            d = sum(BLOCK_DIMS)
            mask = np.ones((d, d), dtype=np.int8)
            off = 0
            for b in BLOCK_DIMS:
                mask[off:off + b, off:off + b] = 0
                off += b
            rows, cols = np.nonzero(mask)
            return (d, rows.astype(np.int32), cols.astype(np.int32))
        d = X.shape[1]
        W = jnp.zeros((d, d), dtype=X.dtype).at[rows, cols].set(w_est)
        return X @ W

    def _L0_ffn_ref(x, gamma, beta, Wr, br, W1, b1, W2, b2):
        import jax, jax.numpy as jnp
        import numpy as np
        E = 8
        K = 2
        D = 256
        H = 512
        DOUT = 256
        EPS = 1e-05
        mu = jnp.mean(x, axis=-1, keepdims=True)
        var = jnp.mean(jnp.square(x - mu), axis=-1, keepdims=True)
        xn = (x - mu) * jax.lax.rsqrt(var + EPS) * gamma + beta
        logits = jnp.einsum('bsd,de->bse', xn, Wr) + br
        top_vals, top_idx = jax.lax.top_k(logits, K)
        w = jax.nn.softmax(top_vals, axis=-1)
        w_full = jnp.einsum('bsk,bske->bse', w, jax.nn.one_hot(top_idx, E, dtype=w.dtype))
        y = jnp.zeros(x.shape[:-1] + (DOUT,), x.dtype)
        for e in range(E):
            h = jax.nn.gelu(jnp.einsum('bsd,dh->bsh', xn, W1[e]) + b1[e], approximate=False)
            y_e = jnp.einsum('bsh,hd->bsd', h, W2[e]) + b2[e]
            y = y + y_e * w_full[..., e, None]
        return y
    x = x + _L0_gnn_ref(_layernorm(x, axis=-1), edge_weight, src, dst)
    x = x + _L0_ffn_ref(_layernorm(x, axis=-1)[None], L0_ffn_gamma, L0_ffn_beta, L0_ffn_Wr, L0_ffn_br, L0_ffn_W1, L0_ffn_b1, L0_ffn_W2, L0_ffn_b2)[0]
    return x

_drawn_inputs = setup_inputs


def setup_inputs(seed=0):
    import zlib

    import numpy as np

    out = dict(_drawn_inputs(seed))
    spreads = {'L0_ffn_br': (0.0, 0.1)}
    factors = {'L0_ffn_gamma': 5.996, 'L0_ffn_beta': 5.055, 'L0_ffn_b1': 8.0, 'L0_ffn_b2': 4.26}
    for name, (base, spread) in spreads.items():
        noise = np.random.default_rng([zlib.crc32(name.encode()), seed]).standard_normal(out[name].shape)
        drawn = base * np.exp(spread * noise) if base else spread * noise
        out[name] = jnp.asarray(drawn.astype(out[name].dtype))
    for name, factor in factors.items():
        out[name] = (out[name] * factor).astype(out[name].dtype)
    return out
```

```python
import numpy as np
import concourse.bass as bass
from concourse import mybir
from contextlib import ExitStack

F32 = mybir.dt.float32
F32R = mybir.dt.float32r
BF16 = mybir.dt.bfloat16
I32 = mybir.dt.int32
U32 = mybir.dt.uint32
ALU = mybir.AluOpType
ACT = mybir.ActivationFunctionType
AX = mybir.AxisListType

P = 128
N, D = 12500, 256
NEDGE = 212500
E, H = 8, 512
EPS = 1e-5
KD, KH = D // P, H // P
EROWS, ECOLS = 125, NEDGE // 125
EBLK = -(-ECOLS // P)
ELAST = ECOLS - (EBLK - 1) * P
PICK = 8
ROUNDS = -(-EBLK * EROWS // PICK)
G = 7
TILES = -(-N // P)
GROUPS = TILES // G
LAST = N - (TILES - 1) * P
CAP = (TILES + 1) * P
NT = 204
SPARE = NT - 2 * N // P
SLOTS = E * CAP + SPARE * P
META = 4
ROW = D + META
NOWHERE = 1.0e6
FLAT = N * D // P
CC = 1000
PIECES = FLAT // CC
CB = 3


def wait_from(engine, sem, value):
    if not isinstance(value, int) or value > 0:
        engine.wait_ge(sem, value)


def used(g, s):
    return G * g + max(s - 1, 0)


def wait_apart(engine, sem, value, apart):
    engine.wait_ge(sem, value)
    engine.sem_inc(apart, 1)


class Steps:

    def __init__(self, engine, sem, start):
        self.engine, self.sem, self.start, self.n = engine, sem, start, 0

    def did(self, ins):
        ins.then_inc(self.sem, 1)
        self.n += 1

    def wait(self, apart=None):
        self.engine.wait_ge(self.sem, self.start + self.n)
        if apart is not None:
            self.engine.sem_inc(apart, 1)

    def then(self, ins):
        self.did(ins)
        self.wait()


def build(nc, x, src, dst, edge_weight, gamma, beta, Wr, br, W1, b1, W2, b2, out):
    ctx = ExitStack()
    with ctx:
        def sb(name, shape, dt):
            return ctx.enter_context(nc.sbuf_tensor(name, shape, dt))

        def sem(name):
            return ctx.enter_context(nc.semaphore(name))

        slots = nc.dram_tensor("slots", [SLOTS, ROW], F32, kind="Internal").ap()
        x1_dram = nc.dram_tensor("x1_dram", [N, D], F32, kind="Internal").ap()
        y_dram = nc.dram_tensor("y_dram", [2 * N, D], F32, kind="Internal").ap()

        w1h = sb("w1h", [P, E, KD, H], F32R)
        w1l = sb("w1l", [P, E, KD, H], F32R)
        w2h = sb("w2h", [P, E, KH, D], F32R)
        w2l = sb("w2l", [P, E, KH, D], F32R)
        b1p = sb("b1p", [P, H], BF16)
        b2p = sb("b2p", [P, D], BF16)
        pick_e = sb("pick_e", [P, E, P], BF16)

        XG = G * D
        arena_x = sb("arena_x", [P, 3 * XG], F32)
        xg = [arena_x[:, b * XG:(b + 1) * XG].rearrange("p (s d) -> p s d", s=G) for b in range(2)]
        xn = arena_x[:, 2 * XG:3 * XG].rearrange("p (s d) -> p s d", s=G)
        stage = [arena_x[:, i * H:(i + 1) * H] for i in range(2)]
        scaled = arena_x[:, 2 * H:3 * H]
        table_id = arena_x[:, XG:XG + KD * D].rearrange("p (k d) -> p k d", k=KD)
        newer = arena_x[:, XG + KD * D:XG + 2 * KD * D].bitcast(I32).rearrange("p (k d) -> p k d", k=KD)
        hot_s = arena_x[:, XG + 2 * KD * D:XG + 2 * KD * D + D]
        hot_d = arena_x[:, XG + 2 * KD * D + D:XG + 2 * KD * D + 3 * D].rearrange("p (a d) -> p a d", a=2)
        diag = arena_x[:, 2 * XG:2 * XG + 2 * P].rearrange("p (a n) -> p a n", a=2)
        later = arena_x[:, 2 * XG + 2 * P:2 * XG + 3 * P]
        arena_z = sb("arena_z", [P, 2 * G * ROW], F32)
        ECT = EBLK * EROWS
        keyT = arena_z[:, 0:ECT]
        wT = arena_z[:, ECT:2 * ECT]
        zg = [arena_z[:, b * G * ROW:(b + 1) * G * ROW].rearrange("p (s d) -> p s d", s=G) for b in range(2)]
        arena_s = sb("arena_s", [P, 2 * ECT], F32)
        score = arena_s[:, 0:ECT]
        junk = arena_s[:, ECT:2 * ECT]
        edge_no = junk.bitcast(I32)
        raw = [arena_x[0:EROWS, 0:ECOLS], arena_x[0:EROWS, ECOLS:2 * ECOLS], junk[0:EROWS, 0:ECOLS]]
        key_raw = raw[0]
        xT = [arena_s[:, i * D:(i + 1) * D] for i in range(2)]
        zT = [arena_s[:, (2 + i) * D:(3 + i) * D] for i in range(2)]
        bpart = arena_s[0:E, 8 * D:8 * D + 3 * (H + D) // 2].bitcast(BF16).rearrange("e (q n) -> e q n", q=3)
        tile_row = arena_s[:, 0:NT]
        tmp_t = arena_s[:, NT:2 * NT]
        betb = arena_x[:, 2 * XG + 4 * P:2 * XG + 6 * P].rearrange("p (k m) -> p k m", k=KD)
        zin = [arena_s[:, 5 * D + i * ROW:5 * D + (i + 1) * ROW] for i in range(2)]
        hact = arena_s[:, 5 * D + 2 * ROW:7 * D + 2 * ROW]
        ysb = [arena_s[:, (7 + i) * D + 2 * ROW:(8 + i) * D + 2 * ROW] for i in range(2)]

        table = sb("table", [P, KD, D], F32)
        ident = sb("ident", [P, P], F32)
        ones = sb("ones", [P, P], F32)
        onesb = sb("onesb", [P, P], BF16)
        before = sb("before", [P, P], BF16)
        iota_d = sb("iota_d", [P, D], F32)
        iota_e = sb("iota_e", [P, E], F32)
        first_e = sb("first_e", [P, E], F32)
        base_e = sb("base_e", [P, E], F32)
        tok = sb("tok", [P, G], F32)
        gam = sb("gam", [P, KD], F32)
        bet = sb("bet", [P, KD], F32)
        wr = sb("wr", [P, KD, E], F32)
        wrg = sb("wrg", [P, KD, E], F32)
        brb = sb("brb", [P, E], F32)
        lbias = sb("lbias", [P, E], F32)
        bet_e = sb("bet_e", [P, KD, E, E], F32)
        b1row = sb("b1row", [E, H], F32)
        b2row = sb("b2row", [E, D], F32)

        top = sb("top", [P, PICK], F32)
        pkey = sb("pkey", [P, PICK], F32)
        pw = sb("pw", [P, PICK], F32)
        pki = sb("pki", [P, PICK], I32)
        psi = sb("psi", [P, PICK], I32)
        pdi = sb("pdi", [P, PICK], I32)
        psf = sb("psf", [P, PICK], F32)
        pdf = sb("pdf", [P, PICK], F32)
        beaten = sb("beaten", [P, 1], F32)
        alive = sb("alive", [P, 1], F32)
        n_edge = sb("n_edge", [P, 1], F32)
        n_maxf = sb("n_maxf", [1, 1], F32)
        n_max = sb("n_max", [1, 1], I32)

        bn6 = sb("bn6", [P, G, 6], F32)
        mv = [sb(f"mv{i}", [P, G, 2], F32) for i in range(2)]
        var_u = sb("var_u", [P, G], F32)
        rs_a = sb("rs_a", [P, G], F32)
        rs = [sb(f"rs{i}", [P, G], F32) for i in range(2)]
        lg = sb("lg", [P, G, E], F32)
        lg2 = sb("lg2", [P, G, E], F32)
        tmp8 = sb("tmp8", [P, G, E], F32)
        oh = sb("oh", [P, 2, G, E], F32)
        best = sb("best", [P, 2, G], F32)
        which = sb("which", [P, 2, G], F32)
        chosen = sb("chosen", [P, G, E], BF16)
        earlier = sb("earlier", [P, G, E], BF16)
        total = sb("total", [P, E], BF16)
        rowok = sb("rowok", [P, 1], F32)
        rank = sb("rank", [P, G, E], F32)
        gap = sb("gap", [P, G], F32)
        egap = sb("egap", [P, G], F32)
        esum = sb("esum", [P, G], F32)
        wtop = sb("wtop", [P, G], F32)
        wsec = sb("wsec", [P, G], F32)
        pos = [sb(f"pos{i}", [P, 2, G], U32) for i in range(2)]

        cnt = sb("cnt", [P, E], F32)
        cnt_i = sb("cnt_i", [P, E], I32)
        tiles_i = sb("tiles_i", [P, E], I32)
        tiles_f = sb("tiles_f", [P, E], F32)
        ends = sb("ends", [P, E], F32)
        jump = sb("jump", [P, E], F32)
        tile_e = sb("tile_e", [P, NT], F32)
        tile_i = sb("tile_i", [1, 2, NT], I32)
        tail_i = sb("tail_i", [1, E], I32)
        filler = sb("filler", [P, ROW], F32)

        xh = [sb(f"xh{i}", [P, D], F32R) for i in range(2)]
        xl = [sb(f"xl{i}", [P, D], F32R) for i in range(2)]
        hh = sb("hh", [P, H], F32R)
        hl = sb("hl", [P, H], F32R)
        second = [sb(f"second{i}", [P, 1], F32) for i in range(2)]
        ywt = [sb(f"ywt{i}", [P, 1], F32) for i in range(2)]
        yid = [sb(f"yid{i}", [P, 1], U32) for i in range(2)]

        bank = [ctx.enter_context(nc.psum_tensor(f"bank{i}", [P, 512], F32)) for i in range(8)]

        s_const = sem("s_const")
        const_step = sem("const_step")
        dve_passed = sem("dve_passed")
        pool_passed = sem("pool_passed")
        raw_in = sem("raw_in")
        small_in = sem("small_in")
        keys_ready = sem("keys_ready")
        block_turned = sem("block_turned")
        block_out = sem("block_out")
        edge_step = sem("edge_step")
        n_edge_ready = sem("n_edge_ready")
        n_edge_turned = sem("n_edge_turned")
        n_max_ready = sem("n_max_ready")
        diag_ready = sem("diag_ready")
        rows_ready = sem("rows_ready")
        hot_ready = sem("hot_ready")
        new_ready = sem("new_ready")
        table_ready = sem("table_ready")

        stage_in = [sem(f"stage_in{i}") for i in range(2)]
        w_high = sem("w_high")
        w_scaled = sem("w_scaled")
        w_low = sem("w_low")
        w_read = sem("w_read")
        b_zeroed = sem("b_zeroed")
        bias_mm = sem("bias_mm")
        bias_step = sem("bias_step")
        bias_split = sem("bias_split")
        bias_in = sem("bias_in")
        lbias_mm = sem("lbias_mm")
        lbias_ready = sem("lbias_ready")
        wrg_ready = sem("wrg_ready")
        scratch_ready = sem("scratch_ready")

        x_in = [sem(f"x_in{i}") for i in range(2)]
        x1_out = [sem(f"x1_out{i}") for i in range(2)]
        norm_step = sem("norm_step")
        xn_ready = sem("xn_ready")
        xT_mm = sem("xT_mm")
        xT_ready = sem("xT_ready")
        g_ready = sem("g_ready")
        g_added = sem("g_added")
        znorm_step = sem("znorm_step")
        z_ready = sem("z_ready")
        zT_mm = sem("zT_mm")
        zT_ready = sem("zT_ready")
        logits_ready = sem("logits_ready")
        route_step = sem("route_step")
        gap_ready = sem("gap_ready")
        egap_ready = sem("egap_ready")
        chosen_ready = sem("chosen_ready")
        rank_ready = sem("rank_ready")
        routed = sem("routed")
        sent = [sem(f"sent{i}") for i in range(2)]

        count_mm = sem("count_mm")
        count_step = sem("count_step")
        tables_ready = sem("tables_ready")
        filled = sem("filled")

        z_in = [sem(f"z_in{i}") for i in range(2)]
        zx_mm = sem("zx_mm")
        xh_ready = sem("xh_ready")
        xl_ready = sem("xl_ready")
        meta_step = sem("meta_step")
        meta_ready = sem("meta_ready")
        h_mm = sem("h_mm")
        h_ready = sem("h_ready")
        hT_mm = sem("hT_mm")
        hh_ready = sem("hh_ready")
        hl_ready = sem("hl_ready")
        y_mm = sem("y_mm")
        y_ready = [sem(f"y_ready{i}") for i in range(2)]
        y_out = [sem(f"y_out{i}") for i in range(2)]

        c_in = [sem(f"c_in{i}") for i in range(CB)]
        c_step = sem("c_step")
        c_ready = sem("c_ready")
        c_out = [sem(f"c_out{i}") for i in range(CB)]

        x_tiled = x[0:(TILES - 1) * P, :].rearrange("(n p) d -> p n d", p=P)
        x1_tiled = x1_dram[0:(TILES - 1) * P, :].rearrange("(n p) d -> p n d", p=P)

        c_x = [arena_x[:, i * CC:(i + 1) * CC] for i in range(CB)]
        c_a = [arena_z[:, i * CC:(i + 1) * CC] for i in range(CB)]
        c_b = [arena_s[:, i * CC:(i + 1) * CC] for i in range(CB)]
        x1_flat = x1_dram.rearrange("n d -> (n d)").rearrange("(p c) -> p c", p=P)
        y_flat = [y_dram[k * N:(k + 1) * N, :].rearrange("n d -> (n d)").rearrange("(p c) -> p c", p=P) for k in range(2)]
        out_flat = out.rearrange("n d -> (n d)").rearrange("(p c) -> p c", p=P)

        block = ctx.enter_context(nc.Block())

        @block.sync
        def _(sp):
            for i, a in enumerate((src, dst, edge_weight)):
                sp.dma_start(raw[i].bitcast(a.dtype), a.rearrange("(p c) -> p c", p=EROWS)).then_inc(raw_in, 16)
            sp.dma_start(wr[:, :, :], Wr.rearrange("(k p) e -> p k e", p=P)).then_inc(small_in, 16)
            with nc.allow_non_contiguous_dma(reason="two values a partition"):
                sp.dma_start(gam[:, :], gamma.rearrange("(k p) -> p k", p=P)).then_inc(small_in, 16)
                sp.dma_start(bet[:, :], beta.rearrange("(k p) -> p k", p=P)).then_inc(small_in, 16)
            sp.dma_start(brb[:, :], br.rearrange("(a e) -> a e", a=1).to_broadcast([P, E])).then_inc(small_in, 16)
            sp.dma_start(b1row[:, :], b1).then_inc(small_in, 16)
            sp.dma_start(b2row[:, :], b2).then_inc(small_in, 16)
            sp.wait_ge(block_turned, 2 * EBLK)
            with sp.Fori(0, E) as e:
                for k in range(KD):
                    sp.wait_ge(w_read, 2 * e)
                    sp.wait_ge(w_low, 2 * e)
                    sp.dma_start(stage[k], W1[bass.ds(e, 1), k * P:(k + 1) * P, :].rearrange("a p h -> p (a h)")).then_inc(stage_in[k], 16)
            with sp.Fori(0, E) as e:
                for k in range(2):
                    sp.wait_ge(w_low, 2 * e + 2 * E)
                    if k == 0:
                        sp.wait_ge(w_read, 2 * E)
                    sp.dma_start(stage[k].rearrange("p (k d) -> p k d", k=2),
                                 W2[bass.ds(e, 1), 2 * k * P:2 * (k + 1) * P, :].rearrange("a (k p) d -> p (a k) d", p=P)).then_inc(stage_in[k], 16)

            def load_x(g, b, full=True):
                if full:
                    sp.dma_start(xg[b][:, :, :], x_tiled[:, bass.ds(g * G, G), :]).then_inc(x_in[b], 16)
                else:
                    sp.dma_start(xg[b][:, 0:G - 1, :], x_tiled[:, g * G:g * G + G - 1, :]).then_inc(x_in[b], 16)
                    sp.dma_start(xg[b][0:LAST, G - 1, :], x[(TILES - 1) * P:N, :]).then_inc(x_in[b], 16)

            def turn_over(g, b, i, full=True):
                sp.wait_ge(g_added, G * (g + 1))
                sp.dma_start(x1_tiled[:, bass.ds(g * G, G), :], xg[b][:, :, :]).then_inc(x1_out[b], 16)
                sp.wait_ge(x1_out[b], 16 * (i + 1))
                sp.wait_ge(z_ready, G * (g + 1))
                load_x(g + 2, b, full)

            sp.wait_ge(w_low, 4 * E)
            load_x(0, 0)
            sp.wait_ge(table_ready, 1)
            load_x(1, 1)
            sp.wait_ge(bias_split, 1)
            sp.wait_ge(b_zeroed, 1)
            for q in range(3):
                sp.dma_start(b1p[q * E:(q + 1) * E, :], bpart[:, q, 0:H]).then_inc(bias_in, 16)
                sp.dma_start(b2p[q * E:(q + 1) * E, :], bpart[:, q, H:H + D]).then_inc(bias_in, 16)
            with sp.Fori(0, GROUPS // 2 - 2) as i:
                for u in range(2):
                    turn_over(2 * i + u, u, i)
            turn_over(GROUPS - 4, 0, GROUPS // 2 - 2)
            turn_over(GROUPS - 3, 1, GROUPS // 2 - 2, full=False)
            sp.wait_ge(g_added, G * (GROUPS - 1))
            sp.dma_start(x1_tiled[:, (GROUPS - 2) * G:(GROUPS - 1) * G, :], xg[0][:, :, :]).then_inc(x1_out[0], 16)
            sp.wait_ge(g_added, G * GROUPS)
            sp.dma_start(x1_tiled[:, (GROUPS - 1) * G:TILES - 1, :], xg[1][:, 0:G - 1, :]).then_inc(x1_out[1], 16)
            sp.dma_start(x1_dram[(TILES - 1) * P:N, :], xg[1][0:LAST, G - 1, :]).then_inc(x1_out[1], 16)

            sp.wait_ge(s_const, 1)
            sp.dma_start(slots[E * CAP:SLOTS, :].rearrange("(n p) d -> p n d", p=P),
                         filler[:, :].unsqueeze(1).to_broadcast([P, SPARE, ROW])).then_inc(filled, 16)
            sp.wait_ge(tables_ready, 1)
            for e in range(E):
                r = sp.value_load(tail_i[0:1, e:e + 1], min_val=0, max_val=E * CAP)
                sp.dma_start(slots[bass.ds(r, P), :], filler[:, :]).then_inc(filled, 16)
            sp.wait_ge(filled, 16 * (E + 1))
            for b in range(2):
                sp.wait_ge(sent[b], 16 * 2 * G * GROUPS // 2)

            def load_z(j, b):
                r = sp.value_load(tile_i[0:1, 1, bass.ds(j, 1)], min_val=0, max_val=SLOTS - P)
                sp.dma_start(zin[b][:, :], slots[bass.ds(r, P), :]).then_inc(z_in[b], 16)

            sp.wait_ge(bias_in, 6 * 16)
            load_z(0, 0)
            load_z(1, 1)
            with sp.Fori(0, NT // 2 - 1) as i:
                for u in range(2):
                    sp.wait_ge(zx_mm, 2 * i + u + 1)
                    sp.wait_ge(meta_ready, 2 * i + u + 1)
                    load_z(2 * i + u + 2, u)

            for q in range(2):
                sp.wait_ge(y_out[q], 16 * NT // 2)
                sp.wait_ge(x1_out[q], 16 * GROUPS // 2 + 16 * q)

            def load_piece(k, b, i):
                sp.wait_ge(c_out[b], 16 * i)
                for buf, flat in ((c_x, x1_flat), (c_a, y_flat[0]), (c_b, y_flat[1])):
                    sp.dma_start(buf[b], flat[:, bass.ds(k * CC, CC)]).then_inc(c_in[b], 16)
            with sp.Fori(0, PIECES // CB) as i:
                for b in range(CB):
                    load_piece(CB * i + b, b, i)
            load_piece(PIECES - 1, 0, PIECES // CB)

        @block.gpsimd
        def _(pool):
            pool.memset(filler[:, 0:D], 0.0)
            pool.memset(filler[:, D + 1:ROW], 0.0)
            pool.memset(filler[:, D:D + 1], NOWHERE).then_inc(s_const, 1)
            pool.memset(ident[:, :], 0.0).then_inc(s_const, 1)
            pool.memset(onesb[:, :], 1.0)
            pool.memset(pick_e[:, :, :], 0.0)
            pool.memset(before[:, :], 1.0).then_inc(s_const, 1)
            pool.wait_ge(s_const, 3)
            pool.affine_select(out=ident[:, :], in_=ident[:, :], compare_op=ALU.not_equal, fill=1.0,
                               base=0, pattern=[[-1, P]], channel_multiplier=1)
            pool.affine_select(out=before[:, :], in_=before[:, :], compare_op=ALU.is_gt, fill=0.0,
                               base=0, pattern=[[1, P]], channel_multiplier=-1)
            pool.memset(ones[:, :], 1.0)
            pool.memset(table[:, :, :], 0.0)
            pool.memset(bet_e[:, :, :, :], 0.0)
            pool.memset(b2p[:, :], 0.0)
            pool.memset(b1p[:, :], 0.0).then_inc(b_zeroed, 1)
            for q in range(3):
                pool.affine_select(out=pick_e[:, :, :], in_=pick_e[:, :, :], compare_op=ALU.not_equal, fill=1.0,
                                   base=-q * E, pattern=[[-1, E], [0, P]], channel_multiplier=1).then_inc(const_step, 1)
                pool.wait_ge(const_step, q + 1)
            pool.memset(arena_z[:, 0:2 * ECT], 0.0)
            pool.memset(total[:, :], 0.0)
            pool.memset(tile_e[:, :], 0.0)
            pool.iota(iota_d[:, :], pattern=[[1, D]], base=0, channel_multiplier=0, allow_small_or_imprecise_dtypes=True)
            pool.iota(iota_e[:, :], pattern=[[1, E]], base=0, channel_multiplier=0, allow_small_or_imprecise_dtypes=True)
            pool.iota(first_e[:, :], pattern=[[-1, E]], base=E, channel_multiplier=0, allow_small_or_imprecise_dtypes=True)
            pool.iota(base_e[:, :], pattern=[[CAP, E]], base=0, channel_multiplier=0, allow_small_or_imprecise_dtypes=True)
            pool.iota(rowok[:, :], pattern=[[0, 1]], base=0, channel_multiplier=1, allow_small_or_imprecise_dtypes=True)
            pool.iota(tok[:, :], pattern=[[P, G]], base=0, channel_multiplier=1, allow_small_or_imprecise_dtypes=True).then_inc(s_const, 1)
            def low(i, k, target, high, scale=None):
                if scale is not None:
                    wait_apart(pool, w_low, 2 * i + k, pool_passed)
                    pool.tensor_scalar(scaled, stage[k], scale, None, ALU.mult).then_inc(w_scaled, 1)
                    pool.wait_ge(w_scaled, 2 * i + k + 1)
                    wait_apart(pool, w_high, 2 * i + k + 1, pool_passed)
                    pool.tensor_tensor(target, scaled, high, ALU.subtract).then_inc(w_low, 1)
                else:
                    wait_apart(pool, w_high, 2 * E + 2 * i + k + 1, pool_passed)
                    pool.tensor_tensor(target, stage[k], high, ALU.subtract).then_inc(w_low, 1)
            pool.wait_ge(small_in, 96)
            pool.wait_ge(block_turned, 2 * EBLK)
            pool.memset(table_id[:, :, :], 0.0)
            pool.iota(edge_no.rearrange("p (b r) -> p b r", b=EBLK), pattern=[[P, EBLK], [ECOLS, EROWS]], base=1, channel_multiplier=1).then_inc(scratch_ready, 1)
            with pool.Fori(0, E) as e:
                for k in range(KD):
                    wait_apart(pool, stage_in[k], 16 * e + 16, pool_passed)
                    low(e, k, w1l[:, bass.ds(e, 1), k, :].rearrange("p a h -> p (a h)"),
                        w1h[:, bass.ds(e, 1), k, :].rearrange("p a h -> p (a h)").bitcast(F32), gam[:, k:k + 1])
            with pool.Fori(0, E) as e:
                for k in range(2):
                    wait_apart(pool, stage_in[k], 16 * e + 16 * E + 16, pool_passed)
                    low(e, k, w2l[:, bass.ds(e, 1), 2 * k:2 * k + 2, :].rearrange("p a k d -> p (a k d)"),
                        w2h[:, bass.ds(e, 1), 2 * k:2 * k + 2, :].rearrange("p a k d -> p (a k d)").bitcast(F32))
            def send(g, b, full=True):
                wait_apart(pool, routed, g + 1, pool_passed)
                for s in range(G):
                    n = P if full or s < G - 1 else LAST
                    for k in range(2):
                        pool.indirect_dma_start(slots[:, :], bass.IndirectOffsetOnAxis(ap=pos[b][0:n, k, s:s + 1], axis=0),
                                                zg[b][0:n, s, :], None).then_inc(sent[b], 16)
            with pool.Fori(0, GROUPS // 2 - 1) as i:
                for u in range(2):
                    send(2 * i + u, u)
            send(GROUPS - 2, 0)
            send(GROUPS - 1, 1, full=False)
            with pool.Fori(0, NT // 2) as i:
                for u in range(2):
                    wait_apart(pool, y_ready[u], i + 1, pool_passed)
                    pool.indirect_dma_start(y_dram[:, :], bass.IndirectOffsetOnAxis(ap=yid[u][:, 0:1], axis=0),
                                            ysb[u][:, :], None, bounds_check=2 * N - 1, oob_is_err=False).then_inc(y_out[u], 16)

        @block.tensor
        def _(pe):
            def wide(b, n):
                return bank[b][:, 0:n]

            pe.wait_ge(s_const, 4)
            pe.wait_ge(raw_in, 48)
            for a in range(2):
                if a == 0:
                    pe.wait_ge(keys_ready, 1)
                for i in range(EBLK):
                    m = P if i < EBLK - 1 else ELAST
                    source = raw[0] if a == 0 else raw[2]
                    nc.tensor.transpose(bank[4 * a + i // 4][0:m, (i % 4) * P:(i % 4) * P + EROWS],
                                        source[:, i * P:i * P + m], ident[0:EROWS, 0:EROWS]).then_inc(block_turned, 1)
            pe.wait_ge(block_out, 8)
            pe.wait_ge(n_edge_ready, 1)
            nc.tensor.transpose(bank[7][0:1, 0:P], n_edge[:, :], ident[:, :]).then_inc(n_edge_turned, 1)
            pe.wait_ge(wrg_ready, 1)
            for k in range(KD):
                last = nc.tensor.matmul(bank[1][:, 0:E], betb[:, k, :], wr[:, k, :], start=(k == 0), stop=(k == KD - 1))
            last.then_inc(lbias_mm, 1)
            for e in range(E):
                for k in range(KD):
                    pe.wait_ge(stage_in[k], 16 * e + 16)
                    nc.tensor.matmul(bank[0][0:E, :], bet_e[:, k, e, :], stage[k], start=(e + k == 0),
                                     stop=(e == E - 1 and k == KD - 1)).then_inc(w_read, 1)
            pe.wait_ge(n_max_ready, 1)
            most = pe.value_load(n_max[0:1, 0:1], min_val=0, max_val=ECT)

            def pick(c):
                pe.wait_ge(diag_ready, c + 1)
                nc.tensor.matmul(bank[4][:, 0:2 * P], ones[:, :], diag[:, :, :].rearrange("p a n -> p (a n)"),
                                 start=True, stop=True).then_inc(rows_ready, 1)
                pe.wait_ge(hot_ready, c + 1)
                for m in range(KD):
                    last = nc.tensor.matmul(bank[5 + m][:, :], hot_s[:, m * P:(m + 1) * P],
                                            hot_d[:, :, :].rearrange("p a n -> p (a n)"), start=True, stop=True)
                last.then_inc(new_ready, 1)
            for j in range(PICK):
                pick(j)
            with pe.If(most > PICK):
                with pe.Fori(1, ROUNDS) as r:
                    with pe.If(most > PICK * r):
                        for j in range(PICK):
                            pick(PICK * r + j)

            def turn_x(g, s):
                c = G * g + s
                pe.wait_ge(xn_ready, c + 1)
                for k in range(KD):
                    last = nc.tensor.transpose(bank[s % 2][:, k * P:(k + 1) * P], xn[:, s, k * P:(k + 1) * P], ident[:, :])
                last.then_inc(xT_mm, 1)

            def edge_product(g, s):
                c = G * g + s
                pe.wait_ge(xT_ready, c + 1)
                wait_from(pe, g_added, used(g, s))
                for k in range(KD):
                    last = nc.tensor.matmul(bank[2 + s % 2][:, 0:D], xT[s % 2][:, k * P:(k + 1) * P], table[:, k, :],
                                            start=(k == 0), stop=(k == KD - 1))
                last.then_inc(g_ready, 1)

            def edges(g):
                for s in range(G):
                    turn_x(g, s)
                    if s > 0:
                        edge_product(g, s - 1)
                edge_product(g, G - 1)

            def router(g, b):
                def logits(s):
                    pe.wait_ge(zT_ready, G * g + s + 1)
                    for k in range(KD):
                        last = nc.tensor.matmul(bank[6][:, s * E:(s + 1) * E], zT[s % 2][:, k * P:(k + 1) * P], wrg[:, k, :],
                                                start=(k == 0), stop=(k == KD - 1))
                    last.then_inc(logits_ready, 1)
                for s in range(G):
                    pe.wait_ge(z_ready, G * g + s + 1)
                    for k in range(KD):
                        last = nc.tensor.transpose(bank[4 + s % 2][:, k * P:(k + 1) * P], zg[b][:, s, k * P:(k + 1) * P], ident[:, :])
                    last.then_inc(zT_mm, 1)
                    if s > 0:
                        logits(s - 1)
                logits(G - 1)
                pe.wait_ge(chosen_ready, g + 1)
                nc.tensor.matmul(bank[7][:, 0:G * E], before[:, :], chosen[:, :, :].rearrange("p s e -> p (s e)"), start=True, stop=False)
                nc.tensor.matmul(bank[7][:, 0:G * E], onesb[:, :], earlier[:, :, :].rearrange("p s e -> p (s e)"),
                                 start=False, stop=True).then_inc(rank_ready, 1)

            pe.wait_ge(table_ready, 1)
            pe.wait_ge(lbias_ready, 1)
            pe.wait_ge(bias_split, 1)
            edges(0)
            with pe.Fori(0, GROUPS // 2 - 1) as i:
                for u in range(2):
                    router(2 * i + u, u)
                    edges(2 * i + u + 1)
            router(GROUPS - 2, 0)
            edges(GROUPS - 1)
            router(GROUPS - 1, 1)
            pe.wait_ge(routed, GROUPS)
            nc.tensor.matmul(bank[6][:, 0:E], onesb[:, :], total[:, :], start=True, stop=True).then_inc(count_mm, 1)

            pe.wait_ge(tables_ready, 1)
            pe.wait_ge(w_low, 4 * E)
            pe.wait_ge(bias_in, 6 * 16)

            def turn_z(j, b):
                pe.wait_ge(z_in[b], 8 * (j - b) + 16)
                wait_from(pe, xl_ready, j - 1)
                for k in range(KD):
                    last = nc.tensor.transpose(bank[b][:, k * P:(k + 1) * P], zin[b][:, k * P:(k + 1) * P], ident[:, :])
                last.then_inc(zx_mm, 1)

            def up(j, b):
                e = pe.value_load(tile_i[0:1, 0, bass.ds(j, 1)], min_val=0, max_val=E - 1)
                pe.wait_ge(xl_ready, j + 1)
                wait_from(pe, h_ready, j - 1)
                o = bank[2 + b][:, :]
                nc.tensor.matmul(o, pick_e[:, bass.ds(e, 1), :].rearrange("p a m -> p (a m)"), b1p[:, :], start=True, stop=False)
                for k in range(KD):
                    for xs, ws in ((xh, w1h), (xh, w1l), (xl, w1h)):
                        last = nc.tensor.matmul(o, xs[b][:, k * P:(k + 1) * P], ws[:, bass.ds(e, 1), k, :].rearrange("p a h -> p (a h)"),
                                                start=False, stop=(k == KD - 1 and xs is xl))
                last.then_inc(h_mm, 1)

            def turn_h(j, b):
                pe.wait_ge(h_ready, j + 1)
                wait_from(pe, hl_ready, j - 1)
                for k in range(KH):
                    last = nc.tensor.transpose(bank[4 + b][:, k * P:(k + 1) * P], hact[:, k * P:(k + 1) * P], ident[:, :])
                last.then_inc(hT_mm, 1)

            def down(j, b, i):
                e = pe.value_load(tile_i[0:1, 0, bass.ds(j, 1)], min_val=0, max_val=E - 1)
                pe.wait_ge(hl_ready, j + 1)
                wait_from(pe, y_ready[b], i)
                o = bank[6 + b][:, 0:D]
                nc.tensor.matmul(o, pick_e[:, bass.ds(e, 1), :].rearrange("p a m -> p (a m)"), b2p[:, :], start=True, stop=False)
                for k in range(KH):
                    for hs, ws in ((hh, w2h), (hh, w2l), (hl, w2h)):
                        last = nc.tensor.matmul(o, hs[:, k * P:(k + 1) * P], ws[:, bass.ds(e, 1), k, :].rearrange("p a h -> p (a h)"),
                                                start=False, stop=(k == KH - 1 and hs is hl))
                last.then_inc(y_mm, 1)

            turn_z(0, 0)
            turn_z(1, 1)
            up(0, 0)
            turn_h(0, 0)
            with pe.Fori(0, NT // 2 - 1) as i:
                j = 2 * i
                turn_z(j + 2, 0)
                up(j + 1, 1)
                down(j, 0, i)
                turn_h(j + 1, 1)
                turn_z(j + 3, 1)
                up(j + 2, 0)
                down(j + 1, 1, i)
                turn_h(j + 2, 0)
            up(NT - 1, 1)
            down(NT - 2, 0, NT // 2 - 1)
            turn_h(NT - 1, 1)
            down(NT - 1, 1, NT // 2 - 1)

        @block.vector
        def _(dve):
            v = nc.vector
            dve.wait_ge(raw_in, 48)
            t = Steps(dve, edge_step, 0)
            inside = score[0:EROWS, 0:ECOLS]
            src_i, dst_i = raw[0].bitcast(I32), raw[1].bitcast(I32)
            t.then(v.tensor_tensor(inside, src_i, dst_i, ALU.max))
            t.did(v.tensor_scalar(inside, inside, float(D), None, ALU.is_lt))
            t.then(v.scalar_tensor_tensor(out=key_raw, in0=src_i, scalar=float(D), in1=dst_i, op0=ALU.mult, op1=ALU.add))
            v.scalar_tensor_tensor(out=key_raw, in0=key_raw, scalar=1.0, in1=inside,
                                   op0=ALU.add, op1=ALU.mult).then_inc(keys_ready, 1)
            dve.wait_ge(block_out, 8)
            dve.wait_ge(s_const, 4)
            dve.wait_ge(scratch_ready, 1)
            dve.wait_ge(small_in, 96)
            for k in range(KD):
                v.tensor_scalar(wrg[:, k, :], wr[:, k, :], gam[:, k:k + 1], None, ALU.mult)
                v.tensor_copy(bet_e[:, k, :, :].rearrange("p a b -> p (a b)")[:, 0:E * E:E + 1], bet[:, k:k + 1].to_broadcast([P, E]))
                last = v.tensor_scalar(betb[:, k, :], ones[:, :], bet[:, k:k + 1], None, ALU.mult)
            last.then_inc(wrg_ready, 1)
            t.did(v.scalar_tensor_tensor(out=score, in0=keyT, scalar=0.0, in1=edge_no, op0=ALU.is_gt, op1=ALU.mult))
            t.wait()
            v.tensor_scalar(junk, keyT, 0.0, None, ALU.is_gt, ALU.add, accum_out=n_edge[:, :]).then_inc(n_edge_ready, 1)
            dve.wait_ge(n_edge_turned, 1)
            t.then(v.tensor_reduce(n_maxf[:, :], bank[7][0:1, 0:P], AX.X, ALU.max))
            v.tensor_copy(n_max[:, :], n_maxf[:, :]).then_inc(n_max_ready, 1)
            dve.wait_ge(n_max_ready, 1)
            most = dve.value_load(n_max[0:1, 0:1], min_val=0, max_val=ECT)
            edge_before = t.n

            def pick_round(c0, start):
                t = Steps(dve, edge_step, start)
                t.then(v.max(top[:, :], score))
                for j in range(PICK):
                    for values, picked in ((keyT, pkey), (wT, pw)):
                        t.did(v.scalar_tensor_tensor(out=junk, in0=score, scalar=top[:, j:j + 1], in1=values,
                                                     op0=ALU.is_equal, op1=ALU.mult, accum_out=picked[:, j:j + 1]))
                        t.wait(apart=dve_passed if j == PICK - 1 and picked is pw else None)
                t.did(v.match_replace(out=score, in_to_replace=top[:, :], in_values=score, imm_value=0.0))
                t.then(v.tensor_scalar(pki[:, :], pkey[:, :], 1.0, None, ALU.subtract))
                t.did(v.tensor_scalar(psi[:, :], pki[:, :], 8, None, ALU.arith_shift_right))
                t.then(v.tensor_scalar(pdi[:, :], pki[:, :], D - 1, None, ALU.bitwise_and))
                t.did(v.tensor_copy(psf[:, :], psi[:, :]))
                t.then(v.tensor_copy(pdf[:, :], pdi[:, :]))
                for j in range(PICK):
                    col = slice(j, j + 1)
                    v.tensor_scalar(diag[:, 0, :], ident[:, :], pkey[:, col], None, ALU.mult)
                    v.tensor_scalar(diag[:, 1, :], ident[:, :], top[:, col], None, ALU.mult).then_inc(diag_ready, 1)
                    dve.wait_ge(rows_ready, c0 + j + 1)
                    t.then(v.tensor_scalar(later[:, :], bank[4][:, P:2 * P], top[:, col], None, ALU.is_gt))
                    t.then(v.scalar_tensor_tensor(out=later[:, :], in0=bank[4][:, 0:P], scalar=pkey[:, col], in1=later[:, :],
                                                  op0=ALU.is_equal, op1=ALU.mult, accum_out=beaten[:, :]))
                    t.then(v.tensor_scalar(alive[:, :], beaten[:, :], 0.0, None, ALU.is_equal))
                    v.tensor_scalar(hot_s[:, :], iota_d[:, :], psf[:, col], alive[:, :], ALU.is_equal, ALU.mult)
                    v.tensor_scalar(hot_d[:, 0, :], iota_d[:, :], pdf[:, col], pw[:, col], ALU.is_equal, ALU.mult)
                    v.tensor_scalar(hot_d[:, 1, :], iota_d[:, :], pdf[:, col], top[:, col], ALU.is_equal, ALU.mult).then_inc(hot_ready, 1)
                    dve.wait_ge(new_ready, c0 + j + 1)
                    for m in range(KD):
                        t.did(v.tensor_tensor(newer[:, m, :], bank[5 + m][:, D:2 * D], table_id[:, m, :], ALU.is_gt))
                    t.wait(apart=dve_passed)
                    for m in range(KD):
                        t.did(v.copy_predicated(table[:, m, :], newer[:, m, :], bank[5 + m][:, 0:D]))
                        t.did(v.tensor_tensor(table_id[:, m, :], bank[5 + m][:, D:2 * D], table_id[:, m, :], ALU.max))
                return t.n
            per_round = pick_round(0, edge_before)
            with dve.If(most > PICK):
                with dve.Fori(1, ROUNDS) as r:
                    with dve.If(most > PICK * r):
                        pick_round(PICK * r, edge_before + per_round * r)
            v.memset(gap[:, :], 0.0).then_inc(table_ready, 1)
            v.tensor_tensor(lbias[:, :], bank[1][:, 0:E], brb[:, :], ALU.add).then_inc(lbias_ready, 1)
            t = Steps(dve, bias_step, 0)
            dve.wait_ge(w_read, 2 * E)
            t.then(v.tensor_tensor(b1row[:, :], bank[0][0:E, :], b1row[:, :], ALU.add))
            for q in range(3):
                t.did(v.tensor_copy(bpart[:, q, 0:H], b1row[:, :]))
                last = v.tensor_copy(bpart[:, q, H:H + D], b2row[:, :])
                if q < 2:
                    t.then(last)
                    t.did(v.tensor_tensor(b1row[:, :], b1row[:, :], bpart[:, q, 0:H], ALU.subtract))
                    t.then(v.tensor_tensor(b2row[:, :], b2row[:, :], bpart[:, q, H:H + D], ALU.subtract))
            last.then_inc(bias_split, 1)

            def rsqrt(t, out_, var, a, c):
                t.then(v.tensor_scalar(var_u[:, :], var, a, c, ALU.mult, ALU.add))
                t.then(v.tensor_scalar(rs_a[:, :].bitcast(I32), var_u[:, :].bitcast(I32), 1, None, ALU.arith_shift_right))
                t.then(v.tensor_scalar(out_[:, :].bitcast(I32), rs_a[:, :].bitcast(I32), -1.0, float(0x5f3759df), ALU.mult, ALU.add))
                for _ in range(3):
                    t.then(v.tensor_tensor(rs_a[:, :], out_[:, :], out_[:, :], ALU.mult))
                    t.then(v.scalar_tensor_tensor(out=rs_a[:, :], in0=rs_a[:, :], scalar=-0.5, in1=var_u[:, :], op0=ALU.mult, op1=ALU.mult))
                    t.then(v.scalar_tensor_tensor(out=out_[:, :], in0=rs_a[:, :], scalar=1.5, in1=out_[:, :], op0=ALU.add, op1=ALU.mult))

            def norm_x(g, b, start, loads=1):
                t = Steps(dve, norm_step, start)
                dve.wait_ge(x_in[b], 8 * (g - b) + 16 * loads)
                for s in range(G):
                    t.did(v.bn_stats(bn6[:, s, :], xg[b][:, s, :]))
                t.wait(apart=dve_passed)
                for s in range(G):
                    t.did(v.bn_aggr(mv[0][:, s, :], bn6[:, s, :]))
                t.wait()
                rsqrt(t, rs[0], mv[0][:, :, 1], 1.0, EPS)
                for s in range(G):
                    if s == 0:
                        wait_from(dve, xT_mm, G * g)
                    v.tensor_scalar(xn[:, s, :], xg[b][:, s, :], mv[0][:, s, 0:1], rs[0][:, s:s + 1], ALU.subtract, ALU.mult).then_inc(xn_ready, 1)
                return t.n

            def add_norm_z(g, b, start):
                t = Steps(dve, znorm_step, start)
                for s in range(G):
                    dve.wait_ge(g_ready, G * g + s + 1)
                    v.tensor_tensor(xg[b][:, s, :], bank[2 + s % 2][:, 0:D], xg[b][:, s, :], ALU.add).then_inc(g_added, 1)
                    if s > 0:
                        dve.wait_ge(g_added, G * g + s)
                        t.did(v.bn_stats(bn6[:, s - 1, :], xg[b][:, s - 1, :]))
                dve.wait_ge(g_added, G * g + G)
                t.did(v.bn_stats(bn6[:, G - 1, :], xg[b][:, G - 1, :]))
                t.wait(apart=dve_passed)
                for s in range(G):
                    t.did(v.bn_aggr(mv[1][:, s, :], bn6[:, s, :]))
                t.wait()
                rsqrt(t, rs[1], mv[1][:, :, 1], 1.0 + EPS, EPS * EPS)
                wait_from(dve, sent[b], 16 * G * (g - b))
                for s in range(G):
                    v.tensor_scalar(zg[b][:, s, 0:D], xg[b][:, s, :], mv[1][:, s, 0:1], rs[1][:, s:s + 1], ALU.subtract, ALU.mult).then_inc(z_ready, 1)
                return t.n

            def route(g, b, start, full=True):
                t = Steps(dve, route_step, start)

                def over_tiles(a):
                    return a.unsqueeze(1).to_broadcast([P, G, E])

                def over_experts(a):
                    return a.unsqueeze(2).to_broadcast([P, G, E])
                dve.wait_ge(logits_ready, G * g + G)
                t.then(v.tensor_tensor(lg[:, :, :], bank[6][:, 0:G * E].rearrange("p (s e) -> p s e", s=G), over_tiles(lbias[:, :]), ALU.add))
                for k, l in ((0, lg), (1, lg2)):
                    t.then(v.tensor_reduce(best[:, k, :], l[:, :, :], AX.X, ALU.max))
                    t.then(v.tensor_tensor(tmp8[:, :, :], l[:, :, :], over_experts(best[:, k, :]), ALU.is_equal))
                    t.then(v.tensor_tensor(tmp8[:, :, :], tmp8[:, :, :], over_tiles(first_e[:, :]), ALU.mult))
                    t.then(v.tensor_reduce(which[:, k, :], tmp8[:, :, :], AX.X, ALU.max))
                    t.then(v.tensor_tensor(oh[:, k, :, :], over_tiles(first_e[:, :]), over_experts(which[:, k, :]), ALU.is_equal))
                    if k == 0:
                        t.then(v.scalar_tensor_tensor(out=lg2[:, :, :], in0=oh[:, 0, :, :], scalar=-3.0e38, in1=lg[:, :, :], op0=ALU.mult, op1=ALU.add))
                v.tensor_tensor(gap[:, :], best[:, 1, :], best[:, 0, :], ALU.subtract).then_inc(gap_ready, 1)
                t.then(v.tensor_tensor(chosen[:, :, :], oh[:, 0, :, :], oh[:, 1, :, :], ALU.add))
                if not full:
                    t.did(v.tensor_scalar(rowok[:, :], rowok[:, :], float(LAST), None, ALU.is_lt))
                    t.wait()
                    t.then(v.tensor_scalar(chosen[:, G - 1, :], chosen[:, G - 1, :], rowok[:, :], None, ALU.mult))
                t.then(v.tensor_copy(earlier[:, 0, :], total[:, :]))
                for s in range(1, G):
                    t.then(v.tensor_tensor(earlier[:, s, :], earlier[:, s - 1, :], chosen[:, s - 1, :], ALU.add))
                v.tensor_tensor(total[:, :], earlier[:, G - 1, :], chosen[:, G - 1, :], ALU.add).then_inc(chosen_ready, 1)
                t.did(v.tensor_copy(zg[b][:, :, D], tok[:, :]))
                t.did(v.tensor_scalar(zg[b][:, :, D + 1], which[:, 0, :], -1.0, float(E), ALU.mult, ALU.add))
                t.then(v.tensor_scalar(tok[:, :], tok[:, :], float(G * P), None, ALU.add))
                dve.wait_ge(egap_ready, g + 1)
                t.then(v.tensor_scalar(esum[:, :], egap[:, :], 1.0, None, ALU.add))
                t.then(v.reciprocal(wtop[:, :], esum[:, :]))
                t.did(v.tensor_copy(zg[b][:, :, D + 2], wtop[:, :]))
                t.then(v.tensor_tensor(wsec[:, :], egap[:, :], wtop[:, :], ALU.mult))
                t.did(v.tensor_tensor(zg[b][:, :, D + 3], wsec[:, :], wtop[:, :], ALU.subtract))
                dve.wait_ge(rank_ready, g + 1)
                t.then(v.tensor_tensor(rank[:, :, :], bank[7][:, 0:G * E].rearrange("p (s e) -> p s e", s=G), over_tiles(base_e[:, :]), ALU.add))
                for k in range(2):
                    t.then(v.tensor_tensor(tmp8[:, :, :], oh[:, k, :, :], rank[:, :, :], ALU.mult))
                    with nc.allow_low_precision(reason="summed in float32, whole numbers below 2^24"):
                        last = v.tensor_reduce(pos[b][:, k, :], tmp8[:, :, :], AX.X, ALU.add)
                    if k == 0:
                        t.then(last)
                last.then_inc(routed, 1)
                return t.n

            cx = norm_x(0, 0, 0)
            cz, cr = 26, 32
            with dve.Fori(0, GROUPS // 2 - 1) as i:
                for u in range(2):
                    g = 2 * i + u
                    nz = add_norm_z(g, u, cz * g)
                    norm_x(g + 1, 1 - u, cx * (g + 1))
                    nr = route(g, u, cr * g)
            assert (nz, nr) == (cz, cr), (nz, nr)
            add_norm_z(GROUPS - 2, 0, cz * (GROUPS - 2))
            norm_x(GROUPS - 1, 1, cx * (GROUPS - 1), loads=2)
            route(GROUPS - 2, 0, cr * (GROUPS - 2))
            add_norm_z(GROUPS - 1, 1, cz * (GROUPS - 1))
            route(GROUPS - 1, 1, cr * (GROUPS - 1), full=False)

            t = Steps(dve, count_step, 0)
            dve.wait_ge(count_mm, 1)
            t.then(v.tensor_copy(cnt[:, :], bank[6][:, 0:E]))
            t.did(v.tensor_tensor(tail_i[:, :], cnt[0:1, :], base_e[0:1, :], ALU.add))
            t.then(v.tensor_scalar(cnt_i[:, :], cnt[:, :], float(P - 1), None, ALU.add))
            t.then(v.tensor_scalar(tiles_i[:, :], cnt_i[:, :], 7, None, ALU.arith_shift_right))
            t.then(v.tensor_copy(tiles_f[:, :], tiles_i[:, :]))
            t.did(v.tensor_tensor_scan(out=ends[:, :], data0=ones[:, 0:E], data1=tiles_f[:, :], initial=0.0, op0=ALU.mult, op1=ALU.add))
            t.did(v.tensor_scalar(jump[:, :], tiles_f[:, :], float(-P), float(CAP), ALU.mult, ALU.add))
            t.then(v.tensor_scalar(tile_row[:, :], iota_d[:, 0:NT], float(P), None, ALU.mult))
            for e in range(E):
                t.did(v.scalar_tensor_tensor(out=tile_e[:, :], in0=iota_d[:, 0:NT], scalar=ends[:, e:e + 1], in1=tile_e[:, :], op0=ALU.is_ge, op1=ALU.add))
                t.then(v.tensor_scalar(tmp_t[:, :], iota_d[:, 0:NT], ends[:, e:e + 1], jump[:, e:e + 1], ALU.is_ge, ALU.mult))
                t.then(v.tensor_tensor(tile_row[:, :], tile_row[:, :], tmp_t[:, :], ALU.add))
            v.tensor_scalar(tile_i[:, 0, :], tile_e[0:1, :], float(E - 1), None, ALU.min)
            v.tensor_copy(tile_i[:, 1, :], tile_row[0:1, :]).then_inc(tables_ready, 1)

            def meta(j, b, i):
                dve.wait_ge(z_in[b], 16 * i + 16)
                wait_from(dve, y_ready[b], i)
                wait_from(dve, y_out[b], 16 * i)
                v.tensor_scalar(second[b][:, :], zin[b][:, D + 1:D + 2], tile_e[:, bass.ds(j, 1)], None, ALU.not_equal).then_inc(meta_step, 1)
                dve.wait_ge(meta_step, j + 1)
                v.scalar_tensor_tensor(out=yid[b][:, :], in0=second[b][:, :], scalar=float(N), in1=zin[b][:, D:D + 1], op0=ALU.mult, op1=ALU.add)
                v.scalar_tensor_tensor(out=ywt[b][:, :], in0=second[b][:, :], scalar=zin[b][:, D + 3:D + 4], in1=zin[b][:, D + 2:D + 3],
                                       op0=ALU.mult, op1=ALU.add).then_inc(meta_ready, 1)

            def x_low(j, b):
                dve.wait_ge(xh_ready, j + 1)
                v.tensor_tensor(xl[b][:, :], bank[b][:, 0:D], xh[b][:, :].bitcast(F32), ALU.subtract).then_inc(xl_ready, 1)

            def h_low(j, b):
                dve.wait_ge(hh_ready, j + 1)
                v.tensor_tensor(hl[:, :], bank[4 + b][:, :], hh[:, :].bitcast(F32), ALU.subtract).then_inc(hl_ready, 1)

            x_low(0, 0)
            x_low(1, 1)
            meta(0, 0, 0)
            h_low(0, 0)
            with dve.Fori(0, NT // 2 - 1) as i:
                j = 2 * i
                x_low(j + 2, 0)
                meta(j + 1, 1, i)
                h_low(j + 1, 1)
                x_low(j + 3, 1)
                meta(j + 2, 0, i + 1)
                h_low(j + 2, 0)
            meta(NT - 1, 1, NT // 2 - 1)
            h_low(NT - 1, 1)

            def add_piece(k, b, i, t):
                dve.wait_ge(c_in[b], 48 * i + 48)
                t.then(v.tensor_tensor(c_a[b], c_a[b], c_b[b], ALU.add))
                v.tensor_tensor(c_x[b], c_a[b], c_x[b], ALU.add).then_inc(c_ready, 1)
            with dve.Fori(0, PIECES // CB) as i:
                t = Steps(dve, c_step, CB * i)
                for b in range(CB):
                    add_piece(CB * i + b, b, i, t)
            add_piece(PIECES - 1, 0, PIECES // CB, Steps(dve, c_step, PIECES - 1))

        @block.scalar
        def _(act):
            def copy(out_, in_):
                return nc.scalar.activation(out_, in_, ACT.Copy)
            act.wait_ge(s_const, 4)
            for a, target in ((0, keyT), (1, wT)):
                tv = target.rearrange("p (b r) -> p b r", b=EBLK)
                for q in range(4):
                    hi = min(4 * q + 4, EBLK)
                    act.wait_ge(block_turned, a * EBLK + hi)
                    full = hi - 4 * q - (1 if q == 3 else 0)
                    bv = bank[4 * a + q][:, :].rearrange("p (b r) -> p b r", b=4)
                    ins = copy(tv[:, 4 * q:4 * q + full, :], bv[:, 0:full, 0:EROWS])
                    if q == 3:
                        ins = copy(tv[0:ELAST, EBLK - 1, :], bv[0:ELAST, full, 0:EROWS])
                    ins.then_inc(block_out, 1)

            with act.Fori(0, E) as e:
                for k in range(KD):
                    act.wait_ge(stage_in[k], 16 * e + 16)
                    nc.scalar.activation(w1h[:, bass.ds(e, 1), k, :].rearrange("p a h -> p (a h)"), stage[k], ACT.Copy,
                                         scale=gam[:, k:k + 1]).then_inc(w_high, 1)
            with act.Fori(0, E) as e:
                for k in range(2):
                    act.wait_ge(stage_in[k], 16 * e + 16 * E + 16)
                    copy(w2h[:, bass.ds(e, 1), 2 * k:2 * k + 2, :].rearrange("p a k d -> p (a k d)"), stage[k]).then_inc(w_high, 1)

            def x_copies(g):
                for s in range(G):
                    act.wait_ge(xT_mm, G * g + s + 1)
                    wait_from(act, g_ready, used(g, s))
                    copy(xT[s % 2], bank[s % 2][:, 0:D]).then_inc(xT_ready, 1)

            def z_copies(g):
                for s in range(G):
                    act.wait_ge(zT_mm, G * g + s + 1)
                    wait_from(act, logits_ready, used(g, s))
                    copy(zT[s % 2], bank[4 + s % 2][:, 0:D]).then_inc(zT_ready, 1)
                act.wait_ge(gap_ready, g + 1)
                nc.scalar.activation(egap[:, :], gap[:, :], ACT.Exp).then_inc(egap_ready, 1)

            x_copies(0)
            with act.Fori(0, GROUPS - 1) as g:
                z_copies(g)
                x_copies(g + 1)
            z_copies(GROUPS - 1)

            def x_high(j, b):
                act.wait_ge(zx_mm, j + 1)
                wait_from(act, h_mm, j - 1)
                copy(xh[b][:, :], bank[b][:, 0:D]).then_inc(xh_ready, 1)

            def gelu(j, b):
                act.wait_ge(h_mm, j + 1)
                wait_from(act, hT_mm, j)
                nc.scalar.activation(hact[:, :], bank[2 + b][:, :], ACT.Gelu).then_inc(h_ready, 1)

            def h_high(j, b):
                act.wait_ge(hT_mm, j + 1)
                wait_from(act, y_mm, j)
                copy(hh[:, :], bank[4 + b][:, :]).then_inc(hh_ready, 1)

            def y_scale(j, b, i):
                act.wait_ge(y_mm, j + 1)
                act.wait_ge(meta_ready, j + 1)
                wait_from(act, y_out[b], 16 * i)
                nc.scalar.activation(ysb[b][:, :], bank[6 + b][:, 0:D], ACT.Copy, scale=ywt[b][:, :]).then_inc(y_ready[b], 1)

            x_high(0, 0)
            x_high(1, 1)
            gelu(0, 0)
            h_high(0, 0)
            with act.Fori(0, NT // 2 - 1) as i:
                j = 2 * i
                x_high(j + 2, 0)
                gelu(j + 1, 1)
                y_scale(j, 0, i)
                h_high(j + 1, 1)
                x_high(j + 3, 1)
                gelu(j + 2, 0)
                y_scale(j + 1, 1, i)
                h_high(j + 2, 0)
            gelu(NT - 1, 1)
            y_scale(NT - 2, 0, NT // 2 - 1)
            h_high(NT - 1, 1)
            y_scale(NT - 1, 1, NT // 2 - 1)

            with act.Fori(0, PIECES // CB) as i:
                for b in range(CB):
                    k = CB * i + b
                    act.wait_ge(c_ready, k + 1)
                    act.dma_start(out_flat[:, bass.ds(k * CC, CC)], c_x[b]).then_inc(c_out[b], 16)
            act.wait_ge(c_ready, PIECES)
            act.dma_start(out_flat[:, (PIECES - 1) * CC:PIECES * CC], c_x[0]).then_inc(c_out[0], 16)
            for b in range(CB):
                act.wait_ge(c_out[b], 16 * (PIECES // CB) + 16 * (b == 0))


_INS = ['x', 'src', 'dst', 'edge_weight', 'L0_ffn_gamma', 'L0_ffn_beta', 'L0_ffn_Wr', 'L0_ffn_br', 'L0_ffn_W1', 'L0_ffn_b1',
        'L0_ffn_W2', 'L0_ffn_b2']


def kernel(**inputs):
    import concourse.bacc as bacc
    from concourse.bass_utils import run_bass_kernel_spmd
    nc = bacc.Bacc("TRN2", target_bir_lowering=False, num_devices=1)
    arrays, args = {}, []
    for name in _INS:
        a = np.ascontiguousarray(inputs[name])
        arrays[f"in_{name}_dram"] = a
        args.append(nc.dram_tensor(f"in_{name}_dram", a.shape, mybir.dt.from_np(a.dtype), kind="ExternalInput").ap())
    args.append(nc.dram_tensor("out_0_dram", (N, D), F32, kind="ExternalOutput").ap())
    build(nc, *args)
    r = run_bass_kernel_spmd(nc, [arrays], core_ids=[0])
    return r.results[0]["out_0_dram"]
```

```python
import numpy as np
import concourse.bass as bass
from concourse import mybir
from contextlib import ExitStack

F32 = mybir.dt.float32
F32R = mybir.dt.float32r
BF16 = mybir.dt.bfloat16
I32 = mybir.dt.int32
U32 = mybir.dt.uint32
ALU = mybir.AluOpType
ACT = mybir.ActivationFunctionType
AX = mybir.AxisListType

P = 128
N, D = 12500, 256
NEDGE = 212500
E, H = 8, 512
EPS = 1e-5
KD, KH = D // P, H // P
EROWS, ECOLS = 125, NEDGE // 125
EBLK = -(-ECOLS // P)
ELAST = ECOLS - (EBLK - 1) * P
PICK = 8
ROUNDS = -(-EBLK * EROWS // PICK)
G = 7
TILES = -(-N // P)
GROUPS = TILES // G
LAST = N - (TILES - 1) * P
CAP = (TILES + 1) * P
NT = 204
SPARE = NT - 2 * N // P
SLOTS = E * CAP + SPARE * P
META = 4
ROW = D + META
NOWHERE = 1.0e6
FLAT = N * D // P
CC = 1000
PIECES = FLAT // CC
ZB = 4
CB = 3


def wait_from(engine, sem, value):
    if not isinstance(value, int) or value > 0:
        engine.wait_ge(sem, value)


def used(g, s):
    return G * g + max(s - 1, 0)


def wait_apart(engine, sem, value, apart):
    engine.wait_ge(sem, value)
    engine.sem_inc(apart, 1)


STATS_FIRST = 26
STATS_STEPS = 41
ROUTE_STEPS = 32


class Steps:

    def __init__(self, engine, sem, start):
        self.engine, self.sem, self.start, self.n = engine, sem, start, 0

    def did(self, ins):
        ins.then_inc(self.sem, 1)
        self.n += 1

    def wait(self, apart=None):
        self.engine.wait_ge(self.sem, self.start + self.n)
        if apart is not None:
            self.engine.sem_inc(apart, 1)

    def then(self, ins):
        self.did(ins)
        self.wait()


def build(nc, x, src, dst, edge_weight, gamma, beta, Wr, br, W1, b1, W2, b2, out):
    ctx = ExitStack()
    with ctx:
        def sb(name, shape, dt):
            return ctx.enter_context(nc.sbuf_tensor(name, shape, dt))

        def sem(name):
            return ctx.enter_context(nc.semaphore(name))

        slots = nc.dram_tensor("slots", [SLOTS, ROW], F32, kind="Internal").ap()
        x1_dram = nc.dram_tensor("x1_dram", [N, D], F32, kind="Internal").ap()
        y_dram = nc.dram_tensor("y_dram", [2 * N, D], F32, kind="Internal").ap()

        w1h = sb("w1h", [P, E, KD, H], F32R)
        w1l = sb("w1l", [P, E, KD, H], F32R)
        w2h = sb("w2h", [P, E, KH, D], F32R)
        w2l = sb("w2l", [P, E, KH, D], F32R)
        b1p = sb("b1p", [P, H], BF16)
        b2p = sb("b2p", [P, D], BF16)
        pick_e = sb("pick_e", [P, E, P], BF16)

        XG = G * D
        arena_x = sb("arena_x", [P, 3 * XG], F32)
        xg = [arena_x[:, b * XG:(b + 1) * XG].rearrange("p (s d) -> p s d", s=G) for b in range(2)]
        xn = arena_x[:, 2 * XG:3 * XG].rearrange("p (s d) -> p s d", s=G)
        stage = [arena_x[:, i * H:(i + 1) * H] for i in range(2)]
        scaled = [arena_x[:, 2 * H:3 * H], arena_x[:, 2 * XG + 4 * D:2 * XG + 4 * D + H]]
        betb = arena_x[:, 3 * H:3 * H + KD * P].rearrange("p (k m) -> p k m", k=KD)
        table_id = arena_x[:, XG:XG + KD * D].rearrange("p (k d) -> p k d", k=KD)
        newer = arena_x[:, XG + KD * D:XG + 2 * KD * D].bitcast(I32).rearrange("p (k d) -> p k d", k=KD)
        hot_s = [arena_x[:, XG + (4 + i) * D:XG + (5 + i) * D] for i in range(2)]
        later = [arena_x[:, XG + 6 * D + i * P:XG + 6 * D + (i + 1) * P] for i in range(2)]
        hot_d = [arena_x[:, 2 * XG + 2 * i * D:2 * XG + 2 * (i + 1) * D].rearrange("p (a d) -> p a d", a=2) for i in range(2)]
        arena_z = sb("arena_z", [P, 2 * G * ROW], F32)
        ECT = EBLK * EROWS
        keyT = arena_z[:, 0:ECT]
        diag_key = arena_z[:, ECT:ECT + PICK * P].rearrange("p (j n) -> p j n", j=PICK)
        zg = [arena_z[:, b * G * ROW:(b + 1) * G * ROW].rearrange("p (s d) -> p s d", s=G) for b in range(2)]
        arena_s = sb("arena_s", [P, 2 * ECT], F32)
        score = arena_s[:, 0:ECT]
        junk = arena_s[:, ECT:2 * ECT]
        edge_no = junk.bitcast(I32)
        raw = [arena_x[0:EROWS, 0:ECOLS], arena_x[0:EROWS, ECOLS:2 * ECOLS]]
        key_raw = raw[0]
        diag_no = junk[:, 0:PICK * P].rearrange("p (j n) -> p j n", j=PICK)
        xT = [arena_s[:, i * D:(i + 1) * D] for i in range(2)]
        zT = [arena_s[:, (2 + i) * D:(3 + i) * D] for i in range(2)]
        bpart = arena_s[0:E, 9 * D:9 * D + 3 * (H + D) // 2].bitcast(BF16).rearrange("e (q n) -> e q n", q=3)
        tile_row = arena_s[:, 0:NT]
        tmp_t = arena_s[:, NT:2 * NT]
        zin = [arena_s[:, 4 * D + i * ROW:4 * D + (i + 1) * ROW] for i in range(ZB)]
        EO = 4 * D + ZB * ROW
        hact = arena_s[:, EO:EO + H]
        ysb = [arena_s[:, EO + H + i * D:EO + H + (i + 1) * D] for i in range(2)]

        table = sb("table", [P, KD, D], F32)
        ident = sb("ident", [P, P], F32)
        ones = sb("ones", [P, P], F32)
        onesb = sb("onesb", [P, P], BF16)
        before = sb("before", [P, P], BF16)
        iota_d = sb("iota_d", [P, D], F32)
        iota_e = sb("iota_e", [P, E], F32)
        first_e = sb("first_e", [P, E], F32)
        base_e = sb("base_e", [P, E], F32)
        tok = sb("tok", [P, G], F32)
        gam = sb("gam", [P, KD], F32)
        bet = sb("bet", [P, KD], F32)
        wr = sb("wr", [P, KD, E], F32)
        wrg = sb("wrg", [P, KD, E], F32)
        brb = sb("brb", [P, E], F32)
        lbias = sb("lbias", [P, E], F32)
        bet_e = sb("bet_e", [P, KD, E, E], F32)
        b1row = sb("b1row", [E, H], F32)
        b2row = sb("b2row", [E, D], F32)

        top = sb("top", [P, PICK], F32)
        pkey = sb("pkey", [P, PICK], F32)
        pw = sb("pw", [P, PICK], F32)
        pki = sb("pki", [P, PICK], I32)
        psi = sb("psi", [P, PICK], I32)
        pdi = sb("pdi", [P, PICK], I32)
        psf = sb("psf", [P, PICK], F32)
        pdf = sb("pdf", [P, PICK], F32)
        wanted = sb("wanted", [P, PICK], U32)
        beaten = sb("beaten", [P, PICK], F32)
        alive = sb("alive", [P, PICK], F32)
        n_edge = sb("n_edge", [P, 1], F32)
        n_maxf = sb("n_maxf", [1, 1], F32)
        n_max = sb("n_max", [1, 1], I32)

        bn6 = sb("bn6", [P, 2, G, 6], F32)
        mv = sb("mv", [P, 2, G, 2], F32)
        var_u = sb("var_u", [P, 2, G], F32)
        rs_a = sb("rs_a", [P, 2, G], F32)
        rs = sb("rs", [P, 2, G], F32)
        shift = sb("shift", [P, G], F32)
        lg = sb("lg", [P, G, E], F32)
        lg2 = sb("lg2", [P, G, E], F32)
        tmp8 = sb("tmp8", [P, G, E], F32)
        oh = sb("oh", [P, 2, G, E], F32)
        best = sb("best", [P, 2, G], F32)
        which = sb("which", [P, 2, G], F32)
        chosen = sb("chosen", [P, G, E], BF16)
        earlier = sb("earlier", [P, G, E], BF16)
        total = sb("total", [P, E], BF16)
        rowok = sb("rowok", [P, 1], F32)
        rank = sb("rank", [P, G, E], F32)
        gap = sb("gap", [P, G], F32)
        egap = sb("egap", [P, G], F32)
        esum = sb("esum", [P, G], F32)
        wtop = sb("wtop", [P, G], F32)
        wsec = sb("wsec", [P, G], F32)
        pos = [sb(f"pos{i}", [P, 2, G], U32) for i in range(2)]

        cnt = sb("cnt", [P, E], F32)
        cnt_i = sb("cnt_i", [P, E], I32)
        tiles_i = sb("tiles_i", [P, E], I32)
        tiles_f = sb("tiles_f", [P, E], F32)
        ends = sb("ends", [P, E], F32)
        jump = sb("jump", [P, E], F32)
        tile_e = sb("tile_e", [P, NT], F32)
        tile_i = sb("tile_i", [1, 2, NT], I32)
        tail_i = sb("tail_i", [1, E], I32)
        filler = sb("filler", [P, ROW], F32)

        xh = [sb(f"xh{i}", [P, D], F32R) for i in range(2)]
        xl = [sb(f"xl{i}", [P, D], F32R) for i in range(2)]
        hh = sb("hh", [P, H], F32R)
        hl = sb("hl", [P, H], F32R)
        second = [sb(f"second{i}", [P, 1], F32) for i in range(2)]
        ywt = [sb(f"ywt{i}", [P, 1], F32) for i in range(2)]
        yid = [sb(f"yid{i}", [P, 1], U32) for i in range(2)]

        psum = ctx.enter_context(nc.psum_tensor("psum", [P, 8, 512], F32))
        bank = [psum[:, i, :] for i in range(8)]

        s_const = sem("s_const")
        const_step = sem("const_step")
        dve_passed = sem("dve_passed")
        pool_passed = sem("pool_passed")
        raw_in = sem("raw_in")
        small_in = sem("small_in")
        keys_ready = sem("keys_ready")
        block_turned = sem("block_turned")
        block_out = sem("block_out")
        edge_step = sem("edge_step")
        n_edge_ready = sem("n_edge_ready")
        n_edge_turned = sem("n_edge_turned")
        n_max_ready = sem("n_max_ready")
        wanted_ready = sem("wanted_ready")
        weights_in = sem("weights_in")
        diag_ready = sem("diag_ready")
        rows_ready = sem("rows_ready")
        hot_ready = sem("hot_ready")
        new_ready = sem("new_ready")
        merged = sem("merged")
        table_ready = sem("table_ready")

        stage_in = [sem(f"stage_in{i}") for i in range(2)]
        w_high = sem("w_high")
        w_scaled = sem("w_scaled")
        w_low = sem("w_low")
        w_read = sem("w_read")
        b_zeroed = sem("b_zeroed")
        bias_mm = sem("bias_mm")
        bias_step = sem("bias_step")
        bias_split = sem("bias_split")
        bias_in = sem("bias_in")
        lbias_mm = sem("lbias_mm")
        lbias_ready = sem("lbias_ready")
        wrg_ready = sem("wrg_ready")
        scratch_ready = sem("scratch_ready")

        x_in = [sem(f"x_in{i}") for i in range(2)]
        x1_out = [sem(f"x1_out{i}") for i in range(2)]
        stats_step = sem("stats_step")
        scale_ready = sem("scale_ready")
        xn_ready = sem("xn_ready")
        xT_mm = sem("xT_mm")
        xT_ready = sem("xT_ready")
        g_ready = sem("g_ready")
        g_added = sem("g_added")
        z_ready = sem("z_ready")
        zT_mm = sem("zT_mm")
        zT_ready = sem("zT_ready")
        logits_ready = sem("logits_ready")
        route_step = sem("route_step")
        gap_ready = sem("gap_ready")
        egap_ready = sem("egap_ready")
        chosen_ready = sem("chosen_ready")
        rank_ready = sem("rank_ready")
        routed = sem("routed")
        sent = [sem(f"sent{i}") for i in range(2)]

        count_mm = sem("count_mm")
        count_step = sem("count_step")
        tables_ready = sem("tables_ready")
        filled = sem("filled")

        z_in = [sem(f"z_in{i}") for i in range(ZB)]
        zx_mm = sem("zx_mm")
        xh_ready = sem("xh_ready")
        xl_ready = sem("xl_ready")
        meta_step = sem("meta_step")
        meta_ready = sem("meta_ready")
        h_mm = sem("h_mm")
        h_ready = sem("h_ready")
        hT_mm = sem("hT_mm")
        hh_ready = sem("hh_ready")
        hl_ready = sem("hl_ready")
        y_mm = sem("y_mm")
        y_ready = [sem(f"y_ready{i}") for i in range(2)]
        y_out = [sem(f"y_out{i}") for i in range(2)]

        c_in = [sem(f"c_in{i}") for i in range(CB)]
        c_step = sem("c_step")
        c_ready = sem("c_ready")
        c_out = [sem(f"c_out{i}") for i in range(CB)]

        x_tiled = x[0:(TILES - 1) * P, :].rearrange("(n p) d -> p n d", p=P)
        x1_tiled = x1_dram[0:(TILES - 1) * P, :].rearrange("(n p) d -> p n d", p=P)

        c_x = [arena_x[:, i * CC:(i + 1) * CC] for i in range(CB)]
        c_a = [arena_z[:, i * CC:(i + 1) * CC] for i in range(CB)]
        c_b = [arena_s[:, i * CC:(i + 1) * CC] for i in range(CB)]
        x1_flat = x1_dram.rearrange("n d -> (n d)").rearrange("(p c) -> p c", p=P)
        y_flat = [y_dram[k * N:(k + 1) * N, :].rearrange("n d -> (n d)").rearrange("(p c) -> p c", p=P) for k in range(2)]
        out_flat = out.rearrange("n d -> (n d)").rearrange("(p c) -> p c", p=P)

        block = ctx.enter_context(nc.Block())

        @block.sync
        def _(sp):
            for i, a in enumerate((src, dst)):
                sp.dma_start(raw[i].bitcast(a.dtype), a.rearrange("(p c) -> p c", p=EROWS)).then_inc(raw_in, 16)
            sp.dma_start(wr[:, :, :], Wr.rearrange("(k p) e -> p k e", p=P)).then_inc(small_in, 16)
            with nc.allow_non_contiguous_dma(reason="two values a partition"):
                sp.dma_start(gam[:, :], gamma.rearrange("(k p) -> p k", p=P)).then_inc(small_in, 16)
                sp.dma_start(bet[:, :], beta.rearrange("(k p) -> p k", p=P)).then_inc(small_in, 16)
            sp.dma_start(brb[:, :], br.rearrange("(a e) -> a e", a=1).to_broadcast([P, E])).then_inc(small_in, 16)
            sp.dma_start(b1row[:, :], b1).then_inc(small_in, 16)
            sp.dma_start(b2row[:, :], b2).then_inc(small_in, 16)
            sp.wait_ge(block_turned, EBLK)

            def load_w1(e):
                for k in range(KD):
                    wait_from(sp, w_read, 2 * e - 1 + k)
                    wait_from(sp, w_high, 4 * e - 2 + 2 * k)
                    sp.dma_start(stage[k], W1[bass.ds(e, 1), k * P:(k + 1) * P, :].rearrange("a p h -> p (a h)")).then_inc(stage_in[k], 16)
            load_w1(0)
            with sp.Fori(1, E) as e:
                load_w1(e)
            with sp.Fori(0, E) as e:
                for k in range(2):
                    if k == 0:
                        sp.wait_ge(w_read, 2 * E)
                        sp.wait_ge(w_high, 4 * E)
                    sp.wait_ge(w_low, 2 * e + 2 * E - 1 + k)
                    sp.dma_start(stage[k].rearrange("p (k d) -> p k d", k=2),
                                 W2[bass.ds(e, 1), 2 * k * P:2 * (k + 1) * P, :].rearrange("a (k p) d -> p (a k) d", p=P)).then_inc(stage_in[k], 16)

            def load_x(g, b, full=True):
                if full:
                    sp.dma_start(xg[b][:, :, :], x_tiled[:, bass.ds(g * G, G), :]).then_inc(x_in[b], 16)
                else:
                    sp.dma_start(xg[b][:, 0:G - 1, :], x_tiled[:, g * G:g * G + G - 1, :]).then_inc(x_in[b], 16)
                    sp.dma_start(xg[b][0:LAST, G - 1, :], x[(TILES - 1) * P:N, :]).then_inc(x_in[b], 16)

            def turn_over(g, b, i, full=True):
                sp.wait_ge(g_added, G * (g + 1))
                sp.dma_start(x1_tiled[:, bass.ds(g * G, G), :], xg[b][:, :, :]).then_inc(x1_out[b], 16)
                sp.wait_ge(x1_out[b], 16 * (i + 1))
                sp.wait_ge(z_ready, G * (g + 1))
                load_x(g + 2, b, full)

            sp.wait_ge(w_low, 4 * E)
            load_x(0, 0)
            sp.wait_ge(table_ready, 1)
            load_x(1, 1)
            sp.wait_ge(bias_split, 1)
            sp.wait_ge(b_zeroed, 1)
            for q in range(3):
                sp.dma_start(b1p[q * E:(q + 1) * E, :], bpart[:, q, 0:H]).then_inc(bias_in, 16)
                sp.dma_start(b2p[q * E:(q + 1) * E, :], bpart[:, q, H:H + D]).then_inc(bias_in, 16)
            with sp.Fori(0, GROUPS // 2 - 2) as i:
                for u in range(2):
                    turn_over(2 * i + u, u, i)
            turn_over(GROUPS - 4, 0, GROUPS // 2 - 2)
            turn_over(GROUPS - 3, 1, GROUPS // 2 - 2, full=False)
            sp.wait_ge(g_added, G * (GROUPS - 1))
            sp.dma_start(x1_tiled[:, (GROUPS - 2) * G:(GROUPS - 1) * G, :], xg[0][:, :, :]).then_inc(x1_out[0], 16)
            sp.wait_ge(g_added, G * GROUPS)
            sp.dma_start(x1_tiled[:, (GROUPS - 1) * G:TILES - 1, :], xg[1][:, 0:G - 1, :]).then_inc(x1_out[1], 16)
            sp.dma_start(x1_dram[(TILES - 1) * P:N, :], xg[1][0:LAST, G - 1, :]).then_inc(x1_out[1], 16)

            sp.wait_ge(s_const, 1)
            sp.dma_start(slots[E * CAP:SLOTS, :].rearrange("(n p) d -> p n d", p=P),
                         filler[:, :].unsqueeze(1).to_broadcast([P, SPARE, ROW])).then_inc(filled, 16)
            sp.wait_ge(tables_ready, 1)
            for e in range(E):
                r = sp.value_load(tail_i[0:1, e:e + 1], min_val=0, max_val=E * CAP)
                sp.dma_start(slots[bass.ds(r, P), :], filler[:, :]).then_inc(filled, 16)
            sp.wait_ge(filled, 16 * (E + 1))
            for b in range(2):
                sp.wait_ge(sent[b], 16 * 2 * G * GROUPS // 2)

            def load_z(i, u):
                r = sp.value_load(tile_i[0:1, 1, bass.ds(4 * i + u, 1)], min_val=0, max_val=SLOTS - P)
                sp.dma_start(zin[u % ZB][:, :], slots[bass.ds(r, P), :]).then_inc(z_in[u % ZB], 16)

            sp.wait_ge(bias_in, 6 * 16)
            for u in range(ZB):
                load_z(0, u)
            with sp.Fori(1, NT // ZB) as i:
                for u in range(ZB):
                    sp.wait_ge(zx_mm, ZB * i + u - 3)
                    sp.wait_ge(meta_ready, ZB * i + u - 3)
                    load_z(i, u)

            for q in range(2):
                sp.wait_ge(y_out[q], 16 * NT // 2)
                sp.wait_ge(x1_out[q], 16 * GROUPS // 2 + 16 * q)

            def load_piece(k, b, i):
                wait_from(sp, c_out[b], 16 * i)
                for buf, flat in ((c_x, x1_flat), (c_a, y_flat[0]), (c_b, y_flat[1])):
                    sp.dma_start(buf[b], flat[:, bass.ds(k * CC, CC)]).then_inc(c_in[b], 16)
            for b in range(CB):
                load_piece(b, b, 0)
            with sp.Fori(1, PIECES // CB) as i:
                for b in range(CB):
                    load_piece(CB * i + b, b, i)
            load_piece(PIECES - 1, 0, PIECES // CB)

        @block.gpsimd
        def _(pool):
            pool.memset(filler[:, 0:D], 0.0)
            pool.memset(filler[:, D + 1:ROW], 0.0)
            pool.memset(filler[:, D:D + 1], NOWHERE).then_inc(s_const, 1)
            pool.memset(ident[:, :], 0.0).then_inc(s_const, 1)
            pool.memset(onesb[:, :], 1.0)
            pool.memset(pick_e[:, :, :], 0.0)
            pool.memset(before[:, :], 1.0).then_inc(s_const, 1)
            pool.wait_ge(s_const, 3)
            pool.affine_select(out=ident[:, :], in_=ident[:, :], compare_op=ALU.not_equal, fill=1.0,
                               base=0, pattern=[[-1, P]], channel_multiplier=1)
            pool.affine_select(out=before[:, :], in_=before[:, :], compare_op=ALU.is_gt, fill=0.0,
                               base=0, pattern=[[1, P]], channel_multiplier=-1)
            pool.memset(ones[:, :], 1.0)
            pool.memset(table[:, :, :], 0.0)
            pool.memset(bet_e[:, :, :, :], 0.0)
            pool.memset(b2p[:, :], 0.0)
            pool.memset(b1p[:, :], 0.0).then_inc(b_zeroed, 1)
            for q in range(3):
                pool.affine_select(out=pick_e[:, :, :], in_=pick_e[:, :, :], compare_op=ALU.not_equal, fill=1.0,
                                   base=-q * E, pattern=[[-1, E], [0, P]], channel_multiplier=1).then_inc(const_step, 1)
                pool.wait_ge(const_step, q + 1)
            pool.memset(keyT, 0.0)
            pool.iota(edge_no.rearrange("p (b r) -> p b r", b=EBLK), pattern=[[P, EBLK], [ECOLS, EROWS]], base=1, channel_multiplier=1)
            pool.memset(total[:, :], 0.0)
            pool.memset(tile_e[:, :], 0.0)
            pool.iota(iota_d[:, :], pattern=[[1, D]], base=0, channel_multiplier=0, allow_small_or_imprecise_dtypes=True)
            pool.iota(iota_e[:, :], pattern=[[1, E]], base=0, channel_multiplier=0, allow_small_or_imprecise_dtypes=True)
            pool.iota(first_e[:, :], pattern=[[-1, E]], base=E, channel_multiplier=0, allow_small_or_imprecise_dtypes=True)
            pool.iota(base_e[:, :], pattern=[[CAP, E]], base=0, channel_multiplier=0, allow_small_or_imprecise_dtypes=True)
            pool.iota(rowok[:, :], pattern=[[0, 1]], base=0, channel_multiplier=1, allow_small_or_imprecise_dtypes=True)
            pool.iota(tok[:, :], pattern=[[P, G]], base=0, channel_multiplier=1, allow_small_or_imprecise_dtypes=True).then_inc(s_const, 1)
            def low(c, target, full, high):
                wait_apart(pool, w_high, c, pool_passed)
                pool.tensor_tensor(target, full, high, ALU.subtract).then_inc(w_low, 1)

            pool.wait_ge(block_turned, EBLK)
            pool.memset(table_id[:, :, :], 0.0).then_inc(scratch_ready, 1)

            def fetch(r):
                wait_apart(pool, wanted_ready, r + 1, pool_passed)
                for j in range(PICK):
                    pool.indirect_dma_start(pw[:, j:j + 1], None, edge_weight.rearrange("(n a) -> n a", a=1),
                                            bass.IndirectOffsetOnAxis(ap=wanted[:, j:j + 1], axis=0)).then_inc(weights_in, 16)
            fetch(0)
            with pool.Fori(0, E) as e:
                for k in range(KD):
                    low(4 * e + 2 * k + 2, w1l[:, bass.ds(e, 1), k, :].rearrange("p a h -> p (a h)"), scaled[k],
                        w1h[:, bass.ds(e, 1), k, :].rearrange("p a h -> p (a h)").bitcast(F32))
            with pool.Fori(0, E) as e:
                for k in range(2):
                    low(4 * E + 2 * e + k + 1, w2l[:, bass.ds(e, 1), 2 * k:2 * k + 2, :].rearrange("p a k d -> p (a k d)"), stage[k],
                        w2h[:, bass.ds(e, 1), 2 * k:2 * k + 2, :].rearrange("p a k d -> p (a k d)").bitcast(F32))
            pool.wait_ge(n_max_ready, 1)
            most = pool.value_load(n_max[0:1, 0:1], min_val=0, max_val=ECT)
            with pool.If(most > PICK):
                with pool.Fori(1, ROUNDS) as r:
                    with pool.If(most > PICK * r):
                        fetch(r)
            def send(g, b, full=True):
                wait_apart(pool, routed, g + 1, pool_passed)
                for s in range(G):
                    n = P if full or s < G - 1 else LAST
                    for k in range(2):
                        pool.indirect_dma_start(slots[:, :], bass.IndirectOffsetOnAxis(ap=pos[b][0:n, k, s:s + 1], axis=0),
                                                zg[b][0:n, s, :], None).then_inc(sent[b], 16)
            with pool.Fori(0, GROUPS // 2 - 1) as i:
                for u in range(2):
                    send(2 * i + u, u)
            send(GROUPS - 2, 0)
            send(GROUPS - 1, 1, full=False)
            with pool.Fori(0, NT // 2) as i:
                for u in range(2):
                    wait_apart(pool, y_ready[u], i + 1, pool_passed)
                    pool.indirect_dma_start(y_dram[:, :], bass.IndirectOffsetOnAxis(ap=yid[u][:, 0:1], axis=0),
                                            ysb[u][:, :], None, bounds_check=2 * N - 1, oob_is_err=False).then_inc(y_out[u], 16)

        @block.tensor
        def _(pe):
            def wide(b, n):
                return bank[b][:, 0:n]

            pe.wait_ge(s_const, 4)
            pe.wait_ge(keys_ready, 1)
            for i in range(EBLK):
                m = P if i < EBLK - 1 else ELAST
                nc.tensor.transpose(bank[i // 4][0:m, (i % 4) * P:(i % 4) * P + EROWS],
                                    key_raw[:, i * P:i * P + m], ident[0:EROWS, 0:EROWS]).then_inc(block_turned, 1)
            pe.wait_ge(block_out, 4)
            pe.wait_ge(n_edge_ready, 1)
            nc.tensor.transpose(bank[5][0:1, 0:P], n_edge[:, :], ident[:, :]).then_inc(n_edge_turned, 1)
            pe.wait_ge(wrg_ready, 1)
            for k in range(KD):
                last = nc.tensor.matmul(bank[6][:, 0:E], betb[:, k, :], wr[:, k, :], start=(k == 0), stop=(k == KD - 1))
            last.then_inc(lbias_mm, 1)
            for e in range(E):
                for k in range(KD):
                    pe.wait_ge(stage_in[k], 16 * e + 16)
                    nc.tensor.matmul(bank[7][0:E, :], bet_e[:, k, e, :], stage[k], start=(e + k == 0),
                                     stop=(e == E - 1 and k == KD - 1)).then_inc(w_read, 1)
            pe.wait_ge(n_max_ready, 1)
            most = pe.value_load(n_max[0:1, 0:1], min_val=0, max_val=ECT)

            def picks(r):
                pe.wait_ge(diag_ready, r + 1)
                for q in range(2):
                    nc.tensor.matmul(bank[q], ones[:, :], diag_key[:, 4 * q:4 * q + 4, :].rearrange("p j n -> p (j n)"), start=True, stop=True)
                    last = nc.tensor.matmul(bank[2 + q], ones[:, :], diag_no[:, 4 * q:4 * q + 4, :].rearrange("p j n -> p (j n)"), start=True, stop=True)
                last.then_inc(rows_ready, 1)
                for j in range(PICK):
                    pe.wait_ge(hot_ready, PICK * r + j + 1)
                    for m in range(KD):
                        last = nc.tensor.matmul(bank[4 * (1 - j % 2) + m], hot_s[j % 2][:, m * P:(m + 1) * P],
                                                hot_d[j % 2].rearrange("p a n -> p (a n)"), start=True, stop=True)
                    last.then_inc(new_ready, 1)
            picks(0)
            with pe.If(most > PICK):
                with pe.Fori(1, ROUNDS) as r:
                    with pe.If(most > PICK * r):
                        picks(r)

            def turn_x(g, s):
                c = G * g + s
                pe.wait_ge(xn_ready, c + 1)
                for k in range(KD):
                    last = nc.tensor.transpose(bank[s % 2][:, k * P:(k + 1) * P], xn[:, s, k * P:(k + 1) * P], ident[:, :])
                last.then_inc(xT_mm, 1)

            def edge_product(g, s):
                c = G * g + s
                pe.wait_ge(xT_ready, c + 1)
                wait_from(pe, g_added, used(g, s))
                for k in range(KD):
                    last = nc.tensor.matmul(bank[2 + s % 2][:, 0:D], xT[s % 2][:, k * P:(k + 1) * P], table[:, k, :],
                                            start=(k == 0), stop=(k == KD - 1))
                last.then_inc(g_ready, 1)

            def edges(g):
                for s in range(G):
                    turn_x(g, s)
                    if s > 0:
                        edge_product(g, s - 1)
                edge_product(g, G - 1)

            def router(g, b):
                def logits(s):
                    pe.wait_ge(zT_ready, G * g + s + 1)
                    for k in range(KD):
                        last = nc.tensor.matmul(bank[6][:, s * E:(s + 1) * E], zT[s % 2][:, k * P:(k + 1) * P], wrg[:, k, :],
                                                start=(k == 0), stop=(k == KD - 1))
                    last.then_inc(logits_ready, 1)
                for s in range(G):
                    pe.wait_ge(z_ready, G * g + s + 1)
                    for k in range(KD):
                        last = nc.tensor.transpose(bank[4 + s % 2][:, k * P:(k + 1) * P], zg[b][:, s, k * P:(k + 1) * P], ident[:, :])
                    last.then_inc(zT_mm, 1)
                    if s > 0:
                        logits(s - 1)
                logits(G - 1)

            def ranks(g):
                pe.wait_ge(chosen_ready, g + 1)
                nc.tensor.matmul(bank[7][:, 0:G * E], before[:, :], chosen[:, :, :].rearrange("p s e -> p (s e)"), start=True, stop=False)
                nc.tensor.matmul(bank[7][:, 0:G * E], onesb[:, :], earlier[:, :, :].rearrange("p s e -> p (s e)"),
                                 start=False, stop=True).then_inc(rank_ready, 1)

            def group(g, b):
                edges(g)
                if not (isinstance(g, int) and g == 0):
                    ranks(g - 1)
                router(g, b)

            pe.wait_ge(table_ready, 1)
            pe.wait_ge(lbias_ready, 1)
            pe.wait_ge(bias_split, 1)
            for g in range(2):
                group(g, g)
            with pe.Fori(1, GROUPS // 2) as i:
                for u in range(2):
                    group(2 * i + u, u)
            ranks(GROUPS - 1)
            pe.wait_ge(routed, GROUPS)
            nc.tensor.matmul(bank[6][:, 0:E], onesb[:, :], total[:, :], start=True, stop=True).then_inc(count_mm, 1)

            pe.wait_ge(tables_ready, 1)
            pe.wait_ge(w_low, 4 * E)
            pe.wait_ge(bias_in, 6 * 16)

            def turn_z(i, u):
                pe.wait_ge(z_in[u % ZB], 16 * (i + u // ZB) + 16)
                wait_from(pe, xl_ready, 4 * i + u - 1)
                for k in range(KD):
                    last = nc.tensor.transpose(bank[u % 2][:, k * P:(k + 1) * P], zin[u % ZB][:, k * P:(k + 1) * P], ident[:, :])
                last.then_inc(zx_mm, 1)

            def up(i, u):
                j, b = 4 * i + u, u % 2
                e = pe.value_load(tile_i[0:1, 0, bass.ds(j, 1)], min_val=0, max_val=E - 1)
                pe.wait_ge(xl_ready, j + 1)
                wait_from(pe, h_ready, j - 1)
                o = bank[2 + b][:, :]
                nc.tensor.matmul(o, pick_e[:, bass.ds(e, 1), :].rearrange("p a m -> p (a m)"), b1p[:, :], start=True, stop=False)
                for k in range(KD):
                    for xs, ws in ((xh, w1h), (xh, w1l), (xl, w1h)):
                        last = nc.tensor.matmul(o, xs[b][:, k * P:(k + 1) * P], ws[:, bass.ds(e, 1), k, :].rearrange("p a h -> p (a h)"),
                                                start=False, stop=(k == KD - 1 and xs is xl))
                last.then_inc(h_mm, 1)

            def turn_h(i, u):
                j, b = 4 * i + u, u % 2
                pe.wait_ge(h_ready, j + 1)
                wait_from(pe, hl_ready, j - 1)
                for k in range(KH):
                    last = nc.tensor.transpose(bank[4 + b][:, k * P:(k + 1) * P], hact[:, k * P:(k + 1) * P], ident[:, :])
                last.then_inc(hT_mm, 1)

            def down(i, u):
                j, b = 4 * i + u, u % 2
                e = pe.value_load(tile_i[0:1, 0, bass.ds(j, 1)], min_val=0, max_val=E - 1)
                pe.wait_ge(hl_ready, j + 1)
                wait_from(pe, y_ready[b], 2 * i + u // 2)
                o = bank[6 + b][:, 0:D]
                nc.tensor.matmul(o, pick_e[:, bass.ds(e, 1), :].rearrange("p a m -> p (a m)"), b2p[:, :], start=True, stop=False)
                for k in range(KH):
                    for hs, ws in ((hh, w2h), (hh, w2l), (hl, w2h)):
                        last = nc.tensor.matmul(o, hs[:, k * P:(k + 1) * P], ws[:, bass.ds(e, 1), k, :].rearrange("p a h -> p (a h)"),
                                                start=False, stop=(k == KH - 1 and hs is hl))
                last.then_inc(y_mm, 1)

            def tile_step(i, u):
                turn_z(i, u + 2)
                up(i, u + 1)
                down(i, u)
                turn_h(i, u + 1)

            turn_z(0, 0)
            turn_z(0, 1)
            up(0, 0)
            turn_h(0, 0)
            for u in range(4):
                tile_step(0, u)
            with pe.Fori(1, NT // 4 - 1) as i:
                for u in range(4):
                    tile_step(i, u)
            last_i = NT // 4 - 1
            tile_step(last_i, 0)
            tile_step(last_i, 1)
            up(last_i, 3)
            down(last_i, 2)
            turn_h(last_i, 3)
            down(last_i, 3)

        @block.vector
        def _(dve):
            v = nc.vector
            dve.wait_ge(raw_in, 32)
            t = Steps(dve, edge_step, 0)
            inside = score[0:EROWS, 0:ECOLS]
            src_i, dst_i = raw[0].bitcast(I32), raw[1].bitcast(I32)
            t.then(v.tensor_tensor(inside, src_i, dst_i, ALU.max))
            t.did(v.tensor_scalar(inside, inside, float(D), None, ALU.is_lt))
            t.then(v.scalar_tensor_tensor(out=key_raw, in0=src_i, scalar=float(D), in1=dst_i, op0=ALU.mult, op1=ALU.add))
            v.scalar_tensor_tensor(out=key_raw, in0=key_raw, scalar=1.0, in1=inside,
                                   op0=ALU.add, op1=ALU.mult).then_inc(keys_ready, 1)
            dve.wait_ge(block_out, 4)
            dve.wait_ge(s_const, 4)
            dve.wait_ge(scratch_ready, 1)
            dve.wait_ge(small_in, 96)
            for k in range(KD):
                v.tensor_scalar(wrg[:, k, :], wr[:, k, :], gam[:, k:k + 1], None, ALU.mult)
                v.tensor_copy(bet_e[:, k, :, :].rearrange("p a b -> p (a b)")[:, 0:E * E:E + 1], bet[:, k:k + 1].to_broadcast([P, E]))
                last = v.tensor_scalar(betb[:, k, :], ones[:, :], bet[:, k:k + 1], None, ALU.mult)
            last.then_inc(wrg_ready, 1)
            t.did(v.scalar_tensor_tensor(out=score, in0=keyT, scalar=0.0, in1=edge_no, op0=ALU.is_gt, op1=ALU.mult))
            t.wait()
            v.tensor_scalar(junk, keyT, 0.0, None, ALU.is_gt, ALU.add, accum_out=n_edge[:, :]).then_inc(n_edge_ready, 1)
            dve.wait_ge(n_edge_turned, 1)
            t.then(v.tensor_reduce(n_maxf[:, :], bank[5][0:1, 0:P], AX.X, ALU.max))
            v.tensor_copy(n_max[:, :], n_maxf[:, :]).then_inc(n_max_ready, 1)
            dve.wait_ge(n_max_ready, 1)
            most = dve.value_load(n_max[0:1, 0:1], min_val=0, max_val=ECT)
            edge_before = t.n

            def over_columns(a):
                return a.unsqueeze(2).to_broadcast([P, PICK, P])

            def pick_round(r, start):
                t = Steps(dve, edge_step, start)
                t.then(v.max(top[:, :], score))
                v.tensor_scalar(wanted[:, :], top[:, :], 1.0, 0.0, ALU.subtract, ALU.max).then_inc(wanted_ready, 1)
                for j in range(PICK):
                    t.did(v.scalar_tensor_tensor(out=junk, in0=score, scalar=top[:, j:j + 1], in1=keyT,
                                                 op0=ALU.is_equal, op1=ALU.mult, accum_out=pkey[:, j:j + 1]))
                    t.wait(apart=dve_passed if j == PICK - 1 else None)
                t.did(v.tensor_tensor(diag_key, ident[:, :].unsqueeze(1).to_broadcast([P, PICK, P]), over_columns(pkey[:, :]), ALU.mult))
                v.tensor_tensor(diag_no, ident[:, :].unsqueeze(1).to_broadcast([P, PICK, P]), over_columns(top[:, :]), ALU.mult).then_inc(diag_ready, 1)
                t.did(v.match_replace(out=score, in_to_replace=top[:, :], in_values=score, imm_value=0.0))
                t.did(v.tensor_scalar(pki[:, :], pkey[:, :], 1.0, None, ALU.subtract))
                t.wait()
                t.did(v.tensor_scalar(psi[:, :], pki[:, :], 8, None, ALU.arith_shift_right))
                t.did(v.tensor_scalar(pdi[:, :], pki[:, :], D - 1, None, ALU.bitwise_and))
                t.wait()
                t.did(v.tensor_copy(psf[:, :], psi[:, :]))
                t.did(v.tensor_copy(pdf[:, :], pdi[:, :]))
                dve.wait_ge(rows_ready, r + 1)
                for j in range(PICK + 1):
                    if j < PICK:
                        t.did(v.tensor_scalar(later[j % 2], bank[2 + j // 4][:, (j % 4) * P:(j % 4 + 1) * P], top[:, j:j + 1], None, ALU.is_gt))
                    if j > 0:
                        a = j - 1
                        t.wait()
                        t.did(v.scalar_tensor_tensor(out=later[a % 2], in0=bank[a // 4][:, (a % 4) * P:(a % 4 + 1) * P], scalar=pkey[:, a:a + 1],
                                                     in1=later[a % 2], op0=ALU.is_equal, op1=ALU.mult, accum_out=beaten[:, a:a + 1]))
                        if j < PICK:
                            t.wait()
                t.wait()
                t.did(v.tensor_scalar(alive[:, :], beaten[:, :], 0.0, None, ALU.is_equal))
                t.wait()
                dve.wait_ge(weights_in, 16 * PICK * r + 16 * PICK)

                def hot(j):
                    v.tensor_scalar(hot_s[j % 2], iota_d[:, :], psf[:, j:j + 1], alive[:, j:j + 1], ALU.is_equal, ALU.mult)
                    v.tensor_scalar(hot_d[j % 2][:, 0, :], iota_d[:, :], pdf[:, j:j + 1], pw[:, j:j + 1], ALU.is_equal, ALU.mult)
                    v.tensor_scalar(hot_d[j % 2][:, 1, :], iota_d[:, :], pdf[:, j:j + 1], top[:, j:j + 1], ALU.is_equal, ALU.mult).then_inc(hot_ready, 1)
                hot(0)
                hot(1)
                for j in range(PICK):
                    b = 4 * (1 - j % 2)
                    t.wait(apart=dve_passed)
                    dve.wait_ge(new_ready, PICK * r + j + 1)
                    t.did(v.tensor_tensor(newer[:, :, :], psum[:, b:b + KD, D:2 * D], table_id[:, :, :], ALU.is_gt))
                    t.did(v.tensor_tensor(table_id[:, :, :], psum[:, b:b + KD, D:2 * D], table_id[:, :, :], ALU.max))
                    t.wait(apart=dve_passed)
                    t.did(v.copy_predicated(table[:, :, :], newer[:, :, :], psum[:, b:b + KD, 0:D]))
                    if j + 2 < PICK:
                        hot(j + 2)
                return t.n
            per_round = pick_round(0, edge_before)
            with dve.If(most > PICK):
                with dve.Fori(1, ROUNDS) as r:
                    with dve.If(most > PICK * r):
                        pick_round(r, edge_before + per_round * r)
            v.memset(gap[:, :], 0.0).then_inc(table_ready, 1)
            v.tensor_tensor(lbias[:, :], bank[6][:, 0:E], brb[:, :], ALU.add).then_inc(lbias_ready, 1)
            t = Steps(dve, bias_step, 0)
            dve.wait_ge(w_read, 2 * E)
            t.then(v.tensor_tensor(b1row[:, :], bank[7][0:E, :], b1row[:, :], ALU.add))
            for q in range(3):
                t.did(v.tensor_copy(bpart[:, q, 0:H], b1row[:, :]))
                last = v.tensor_copy(bpart[:, q, H:H + D], b2row[:, :])
                if q < 2:
                    t.then(last)
                    t.did(v.tensor_tensor(b1row[:, :], b1row[:, :], bpart[:, q, 0:H], ALU.subtract))
                    t.then(v.tensor_tensor(b2row[:, :], b2row[:, :], bpart[:, q, H:H + D], ALU.subtract))
            last.then_inc(bias_split, 1)

            def over_tiles(a):
                return a.unsqueeze(1).to_broadcast([P, G, E])

            def over_experts(a):
                return a.unsqueeze(2).to_broadcast([P, G, E])

            def rsqrt(t, a, fill):
                u, w, r = var_u[:, a, :], rs_a[:, a, :], rs[:, a, :]
                t.wait()
                t.did(v.tensor_scalar(w.bitcast(I32), u.bitcast(I32), 1, None, ALU.arith_shift_right))
                fill()
                t.wait()
                t.did(v.tensor_scalar(r.bitcast(I32), w.bitcast(I32), -1.0, float(0x5f3759df), ALU.mult, ALU.add))
                for _ in range(3):
                    fill()
                    t.wait()
                    t.did(v.tensor_tensor(w, r, r, ALU.mult))
                    fill()
                    t.wait()
                    t.did(v.scalar_tensor_tensor(out=w, in0=w, scalar=-0.5, in1=u, op0=ALU.mult, op1=ALU.mult))
                    fill()
                    t.wait()
                    t.did(v.scalar_tensor_tensor(out=r, in0=w, scalar=1.5, in1=r, op0=ALU.add, op1=ALU.mult))

            def x_scales(t, g):
                t.wait()
                v.scalar_tensor_tensor(out=shift[:, :], in0=mv[:, 1, :, 0], scalar=-1.0, in1=rs[:, 1, :], op0=ALU.mult, op1=ALU.mult).then_inc(scale_ready, 1)

            def x_stats(t, g, b, loads=1):
                dve.wait_ge(x_in[b], 8 * (g - b) + 16 * loads)
                for s in range(G):
                    t.did(v.bn_stats(bn6[:, 1, s, :], xg[b][:, s, :]))

            def route(g, b, full=True):
                t = Steps(dve, route_step, ROUTE_STEPS * g)
                dve.wait_ge(logits_ready, G * g + G)
                t.did(v.tensor_tensor(lg[:, :, :], bank[6][:, 0:G * E].rearrange("p (s e) -> p s e", s=G), over_tiles(lbias[:, :]), ALU.add))
                yield
                for k, l in ((0, lg), (1, lg2)):
                    t.wait()
                    t.did(v.tensor_reduce(best[:, k, :], l[:, :, :], AX.X, ALU.max))
                    yield
                    t.wait()
                    t.did(v.tensor_tensor(tmp8[:, :, :], l[:, :, :], over_experts(best[:, k, :]), ALU.is_equal))
                    yield
                    t.wait()
                    t.did(v.tensor_tensor(tmp8[:, :, :], tmp8[:, :, :], over_tiles(first_e[:, :]), ALU.mult))
                    yield
                    t.wait()
                    t.did(v.tensor_reduce(which[:, k, :], tmp8[:, :, :], AX.X, ALU.max))
                    yield
                    t.wait()
                    t.did(v.tensor_tensor(oh[:, k, :, :], over_tiles(first_e[:, :]), over_experts(which[:, k, :]), ALU.is_equal))
                    yield
                    if k == 0:
                        t.wait()
                        t.did(v.scalar_tensor_tensor(out=lg2[:, :, :], in0=oh[:, 0, :, :], scalar=-3.0e38, in1=lg[:, :, :], op0=ALU.mult, op1=ALU.add))
                        yield
                v.tensor_tensor(gap[:, :], best[:, 1, :], best[:, 0, :], ALU.subtract).then_inc(gap_ready, 1)
                t.wait()
                t.did(v.tensor_tensor(chosen[:, :, :], oh[:, 0, :, :], oh[:, 1, :, :], ALU.add))
                if not full:
                    t.did(v.tensor_scalar(rowok[:, :], rowok[:, :], float(LAST), None, ALU.is_lt))
                    t.wait()
                    t.did(v.tensor_scalar(chosen[:, G - 1, :], chosen[:, G - 1, :], rowok[:, :], None, ALU.mult))
                t.did(v.tensor_copy(earlier[:, 0, :], total[:, :]))
                yield
                for s in range(1, G):
                    t.wait()
                    t.did(v.tensor_tensor(earlier[:, s, :], earlier[:, s - 1, :], chosen[:, s - 1, :], ALU.add))
                    yield
                t.wait()
                v.tensor_tensor(total[:, :], earlier[:, G - 1, :], chosen[:, G - 1, :], ALU.add).then_inc(chosen_ready, 1)
                t.did(v.tensor_copy(zg[b][:, :, D], tok[:, :]))
                t.did(v.tensor_scalar(zg[b][:, :, D + 1], which[:, 0, :], -1.0, float(E), ALU.mult, ALU.add))
                t.wait()
                t.did(v.tensor_scalar(tok[:, :], tok[:, :], float(G * P), None, ALU.add))
                yield
                dve.wait_ge(rank_ready, g + 1)
                t.did(v.tensor_tensor(rank[:, :, :], bank[7][:, 0:G * E].rearrange("p (s e) -> p s e", s=G), over_tiles(base_e[:, :]), ALU.add))
                dve.wait_ge(egap_ready, g + 1)
                t.did(v.tensor_scalar(esum[:, :], egap[:, :], 1.0, None, ALU.add))
                yield
                t.wait()
                t.did(v.reciprocal(wtop[:, :], esum[:, :]))
                t.did(v.tensor_tensor(tmp8[:, :, :], oh[:, 0, :, :], rank[:, :, :], ALU.mult))
                yield
                t.wait()
                t.did(v.tensor_copy(zg[b][:, :, D + 2], wtop[:, :]))
                t.did(v.tensor_tensor(wsec[:, :], egap[:, :], wtop[:, :], ALU.mult))
                with nc.allow_low_precision(reason="summed in float32, whole numbers below 2^24"):
                    t.did(v.tensor_reduce(pos[b][:, 0, :], tmp8[:, :, :], AX.X, ALU.add))
                yield
                t.wait()
                t.did(v.tensor_tensor(zg[b][:, :, D + 3], wsec[:, :], wtop[:, :], ALU.subtract))
                t.did(v.tensor_tensor(tmp8[:, :, :], oh[:, 1, :, :], rank[:, :, :], ALU.mult))
                yield
                t.wait()
                with nc.allow_low_precision(reason="summed in float32, whole numbers below 2^24"):
                    v.tensor_reduce(pos[b][:, 1, :], tmp8[:, :, :], AX.X, ALU.add).then_inc(routed, 1)
                assert t.n == ROUTE_STEPS or not full, t.n

            def group(g, b, first=False, last=False, loads=1):
                t = Steps(dve, stats_step, STATS_STEPS * g + STATS_FIRST)
                router = iter(()) if first else route(g - 1, 1 - b)

                def fill():
                    next(router, None)
                for s in range(G):
                    fill()
                    dve.wait_ge(g_ready, G * g + s + 1)
                    v.tensor_tensor(xg[b][:, s, :], bank[2 + s % 2][:, 0:D], xg[b][:, s, :], ALU.add).then_inc(g_added, 1)
                    fill()
                    if s > 0:
                        dve.wait_ge(g_added, G * g + s)
                        t.did(v.bn_stats(bn6[:, 0, s - 1, :], xg[b][:, s - 1, :]))
                        fill()
                dve.wait_ge(g_added, G * g + G)
                t.did(v.bn_stats(bn6[:, 0, G - 1, :], xg[b][:, G - 1, :]))
                if not last:
                    x_stats(t, g + 1, 1 - b, loads)
                t.wait(apart=dve_passed)
                for a in range(1 if last else 2):
                    for s in range(G):
                        t.did(v.bn_aggr(mv[:, a, s, :], bn6[:, a, s, :]))
                t.wait()
                t.did(v.tensor_scalar(var_u[:, 0, :], mv[:, 0, :, 1], 1.0 + EPS, EPS * EPS, ALU.mult, ALU.add))
                if not last:
                    t.did(v.tensor_scalar(var_u[:, 1, :], mv[:, 1, :, 1], 1.0, EPS, ALU.mult, ALU.add))
                rsqrt(t, slice(0, 1 if last else 2), fill)
                if not last:
                    x_scales(t, g + 1)
                else:
                    t.wait()
                wait_from(dve, sent[b], 16 * G * (g - b))
                for s in range(G):
                    v.tensor_scalar(zg[b][:, s, 0:D], xg[b][:, s, :], mv[:, 0, s, 0:1], rs[:, 0, s:s + 1], ALU.subtract, ALU.mult).then_inc(z_ready, 1)
                for _ in router:
                    pass
                return t.n

            t = Steps(dve, stats_step, 0)
            x_stats(t, 0, 0)
            t.wait()
            for s in range(G):
                t.did(v.bn_aggr(mv[:, 1, s, :], bn6[:, 1, s, :]))
            t.wait()
            t.did(v.tensor_scalar(var_u[:, 1, :], mv[:, 1, :, 1], 1.0, EPS, ALU.mult, ALU.add))
            rsqrt(t, slice(1, 2), lambda: None)
            x_scales(t, 0)
            assert t.n == STATS_FIRST, t.n
            n = group(0, 0, first=True)
            assert n == STATS_STEPS, n
            group(1, 1)
            with dve.Fori(1, GROUPS // 2 - 1) as i:
                for u in range(2):
                    group(2 * i + u, u)
            group(GROUPS - 2, 0, loads=2)
            group(GROUPS - 1, 1, last=True)
            for _ in route(GROUPS - 1, 1, full=False):
                pass

            t = Steps(dve, count_step, 0)
            dve.wait_ge(count_mm, 1)
            t.then(v.tensor_copy(cnt[:, :], bank[6][:, 0:E]))
            t.did(v.tensor_tensor(tail_i[:, :], cnt[0:1, :], base_e[0:1, :], ALU.add))
            t.then(v.tensor_scalar(cnt_i[:, :], cnt[:, :], float(P - 1), None, ALU.add))
            t.then(v.tensor_scalar(tiles_i[:, :], cnt_i[:, :], 7, None, ALU.arith_shift_right))
            t.then(v.tensor_copy(tiles_f[:, :], tiles_i[:, :]))
            t.did(v.tensor_tensor_scan(out=ends[:, :], data0=ones[:, 0:E], data1=tiles_f[:, :], initial=0.0, op0=ALU.mult, op1=ALU.add))
            t.did(v.tensor_scalar(jump[:, :], tiles_f[:, :], float(-P), float(CAP), ALU.mult, ALU.add))
            t.then(v.tensor_scalar(tile_row[:, :], iota_d[:, 0:NT], float(P), None, ALU.mult))
            for e in range(E):
                t.did(v.scalar_tensor_tensor(out=tile_e[:, :], in0=iota_d[:, 0:NT], scalar=ends[:, e:e + 1], in1=tile_e[:, :], op0=ALU.is_ge, op1=ALU.add))
                t.then(v.tensor_scalar(tmp_t[:, :], iota_d[:, 0:NT], ends[:, e:e + 1], jump[:, e:e + 1], ALU.is_ge, ALU.mult))
                t.then(v.tensor_tensor(tile_row[:, :], tile_row[:, :], tmp_t[:, :], ALU.add))
            v.tensor_scalar(tile_i[:, 0, :], tile_e[0:1, :], float(E - 1), None, ALU.min)
            v.tensor_copy(tile_i[:, 1, :], tile_row[0:1, :]).then_inc(tables_ready, 1)

            def meta(i, u):
                j, b = 4 * i + u, u % 2
                z = zin[u % ZB]
                dve.wait_ge(z_in[u % ZB], 16 * (i + u // ZB) + 16)
                wait_from(dve, y_ready[b], 2 * i + u // 2)
                wait_from(dve, y_out[b], 32 * i + 16 * (u // 2))
                v.tensor_scalar(second[b][:, :], z[:, D + 1:D + 2], tile_e[:, bass.ds(j, 1)], None, ALU.not_equal).then_inc(meta_step, 1)
                dve.wait_ge(meta_step, j + 1)
                v.scalar_tensor_tensor(out=yid[b][:, :], in0=second[b][:, :], scalar=float(N), in1=z[:, D:D + 1], op0=ALU.mult, op1=ALU.add)
                v.scalar_tensor_tensor(out=ywt[b][:, :], in0=second[b][:, :], scalar=z[:, D + 3:D + 4], in1=z[:, D + 2:D + 3],
                                       op0=ALU.mult, op1=ALU.add).then_inc(meta_ready, 1)

            def x_low(i, u):
                b = u % 2
                dve.wait_ge(xh_ready, 4 * i + u + 1)
                v.tensor_tensor(xl[b][:, :], bank[b][:, 0:D], xh[b][:, :].bitcast(F32), ALU.subtract).then_inc(xl_ready, 1)

            def h_low(i, u):
                dve.wait_ge(hh_ready, 4 * i + u + 1)
                v.tensor_tensor(hl[:, :], bank[4 + u % 2][:, :], hh[:, :].bitcast(F32), ALU.subtract).then_inc(hl_ready, 1)

            def tile_step(i, u):
                x_low(i, u + 2)
                meta(i, u + 1)
                h_low(i, u + 1)

            x_low(0, 0)
            x_low(0, 1)
            meta(0, 0)
            h_low(0, 0)
            for u in range(4):
                tile_step(0, u)
            with dve.Fori(1, NT // 4 - 1) as i:
                for u in range(4):
                    tile_step(i, u)
            last_i = NT // 4 - 1
            tile_step(last_i, 0)
            tile_step(last_i, 1)
            meta(last_i, 3)
            h_low(last_i, 3)

            def add_piece(k, b, i, t):
                dve.wait_ge(c_in[b], 48 * i + 48)
                t.then(v.tensor_tensor(c_a[b], c_a[b], c_b[b], ALU.add))
                v.tensor_tensor(c_x[b], c_a[b], c_x[b], ALU.add).then_inc(c_ready, 1)
            with dve.Fori(0, PIECES // CB) as i:
                t = Steps(dve, c_step, CB * i)
                for b in range(CB):
                    add_piece(CB * i + b, b, i, t)
            add_piece(PIECES - 1, 0, PIECES // CB, Steps(dve, c_step, PIECES - 1))

        @block.scalar
        def _(act):
            def copy(out_, in_):
                return nc.scalar.activation(out_, in_, ACT.Copy)
            act.wait_ge(s_const, 4)
            tv = keyT.rearrange("p (b r) -> p b r", b=EBLK)
            for q in range(4):
                hi = min(4 * q + 4, EBLK)
                act.wait_ge(block_turned, hi)
                full = hi - 4 * q - (1 if q == 3 else 0)
                bv = bank[q].rearrange("p (b r) -> p b r", b=4)
                ins = copy(tv[:, 4 * q:4 * q + full, :], bv[:, 0:full, 0:EROWS])
                if q == 3:
                    ins = copy(tv[0:ELAST, EBLK - 1, :], bv[0:ELAST, full, 0:EROWS])
                ins.then_inc(block_out, 1)
            act.wait_ge(small_in, 96)
            def high1(e):
                for k in range(KD):
                    act.wait_ge(stage_in[k], 16 * e + 16)
                    nc.scalar.activation(w1h[:, bass.ds(e, 1), k, :].rearrange("p a h -> p (a h)"), stage[k], ACT.Copy,
                                         scale=gam[:, k:k + 1]).then_inc(w_high, 1)
                    wait_from(act, w_low, 2 * e - 1 + k)
                    nc.scalar.activation(scaled[k], stage[k], ACT.Copy, scale=gam[:, k:k + 1]).then_inc(w_high, 1)
            high1(0)
            with act.Fori(1, E) as e:
                high1(e)
            with act.Fori(0, E) as e:
                for k in range(2):
                    act.wait_ge(stage_in[k], 16 * e + 16 * E + 16)
                    copy(w2h[:, bass.ds(e, 1), 2 * k:2 * k + 2, :].rearrange("p a k d -> p (a k d)"), stage[k]).then_inc(w_high, 1)

            def x_norm(g, s, b):
                wait_from(act, xT_mm, G * (g - 1) + s + 1)
                nc.scalar.activation(xn[:, s, :], xg[b][:, s, :], ACT.Identity, scale=rs[:, 1, s:s + 1],
                                     bias=shift[:, s:s + 1]).then_inc(xn_ready, 1)

            def x_copy(g, s):
                act.wait_ge(xT_mm, G * g + s + 1)
                wait_from(act, g_ready, used(g, s))
                copy(xT[s % 2], bank[s % 2][:, 0:D]).then_inc(xT_ready, 1)

            def z_copies(g):
                for s in range(G):
                    act.wait_ge(zT_mm, G * g + s + 1)
                    wait_from(act, logits_ready, used(g, s))
                    copy(zT[s % 2], bank[4 + s % 2][:, 0:D]).then_inc(zT_ready, 1)

            def group(g, b):
                act.wait_ge(scale_ready, g + 1)
                x_norm(g, 0, b)
                if not (isinstance(g, int) and g == 0):
                    z_copies(g - 1)
                for s in range(1, G):
                    x_norm(g, s, b)
                    x_copy(g, s - 1)
                x_copy(g, G - 1)
                if not (isinstance(g, int) and g == 0):
                    exp_gap(g - 1)

            def exp_gap(g):
                act.wait_ge(gap_ready, g + 1)
                nc.scalar.activation(egap[:, :], gap[:, :], ACT.Exp).then_inc(egap_ready, 1)

            for g in range(2):
                group(g, g)
            with act.Fori(1, GROUPS // 2) as i:
                for u in range(2):
                    group(2 * i + u, u)
            z_copies(GROUPS - 1)
            exp_gap(GROUPS - 1)

            def x_high(i, u):
                j, b = 4 * i + u, u % 2
                act.wait_ge(zx_mm, j + 1)
                wait_from(act, h_mm, j - 1)
                copy(xh[b][:, :], bank[b][:, 0:D]).then_inc(xh_ready, 1)

            def gelu(i, u):
                j, b = 4 * i + u, u % 2
                act.wait_ge(h_mm, j + 1)
                wait_from(act, hT_mm, j)
                nc.scalar.activation(hact[:, :], bank[2 + b][:, :], ACT.Gelu).then_inc(h_ready, 1)

            def h_high(i, u):
                j, b = 4 * i + u, u % 2
                act.wait_ge(hT_mm, j + 1)
                wait_from(act, y_mm, j)
                copy(hh[:, :], bank[4 + b][:, :]).then_inc(hh_ready, 1)

            def y_scale(i, u):
                j, b = 4 * i + u, u % 2
                act.wait_ge(y_mm, j + 1)
                act.wait_ge(meta_ready, j + 1)
                wait_from(act, y_out[b], 32 * i + 16 * (u // 2))
                nc.scalar.activation(ysb[b][:, :], bank[6 + b][:, 0:D], ACT.Copy, scale=ywt[b][:, :]).then_inc(y_ready[b], 1)

            def tile_step(i, u):
                x_high(i, u + 2)
                gelu(i, u + 1)
                y_scale(i, u)
                h_high(i, u + 1)

            x_high(0, 0)
            x_high(0, 1)
            gelu(0, 0)
            h_high(0, 0)
            for u in range(4):
                tile_step(0, u)
            with act.Fori(1, NT // 4 - 1) as i:
                for u in range(4):
                    tile_step(i, u)
            last_i = NT // 4 - 1
            tile_step(last_i, 0)
            tile_step(last_i, 1)
            gelu(last_i, 3)
            y_scale(last_i, 2)
            h_high(last_i, 3)
            y_scale(last_i, 3)

            with act.Fori(0, PIECES // CB) as i:
                for b in range(CB):
                    k = CB * i + b
                    act.wait_ge(c_ready, k + 1)
                    act.dma_start(out_flat[:, bass.ds(k * CC, CC)], c_x[b]).then_inc(c_out[b], 16)
            act.wait_ge(c_ready, PIECES)
            act.dma_start(out_flat[:, (PIECES - 1) * CC:PIECES * CC], c_x[0]).then_inc(c_out[0], 16)
            for b in range(CB):
                act.wait_ge(c_out[b], 16 * (PIECES // CB) + 16 * (b == 0))


_INS = ['x', 'src', 'dst', 'edge_weight', 'L0_ffn_gamma', 'L0_ffn_beta', 'L0_ffn_Wr', 'L0_ffn_br', 'L0_ffn_W1', 'L0_ffn_b1',
        'L0_ffn_W2', 'L0_ffn_b2']


def kernel(**inputs):
    import concourse.bacc as bacc
    from concourse.bass_utils import run_bass_kernel_spmd
    nc = bacc.Bacc("TRN2", target_bir_lowering=False, num_devices=1)
    arrays, args = {}, []
    for name in _INS:
        a = np.ascontiguousarray(inputs[name])
        arrays[f"in_{name}_dram"] = a
        args.append(nc.dram_tensor(f"in_{name}_dram", a.shape, mybir.dt.from_np(a.dtype), kind="ExternalInput").ap())
    args.append(nc.dram_tensor("out_0_dram", (N, D), F32, kind="ExternalOutput").ap())
    build(nc, *args)
    r = run_bass_kernel_spmd(nc, [arrays], core_ids=[0])
    return r.results[0]["out_0_dram"]
```

```python
import numpy as np
import concourse.bass as bass
from concourse import mybir
from contextlib import ExitStack

F32 = mybir.dt.float32
F32R = mybir.dt.float32r
BF16 = mybir.dt.bfloat16
I32 = mybir.dt.int32
U32 = mybir.dt.uint32
ALU = mybir.AluOpType
ACT = mybir.ActivationFunctionType
AX = mybir.AxisListType

P = 128
N, D = 12500, 256
NEDGE = 212500
E, H = 8, 512
EPS = 1e-5
KD, KH = D // P, H // P
EROWS, ECOLS = 125, NEDGE // 125
EBLK = -(-ECOLS // P)
ELAST = ECOLS - (EBLK - 1) * P
HALF = 2
EARLY = 1
ROW0 = 9
PICK = 8
ROUNDS = -(-EBLK * EROWS // PICK)
G = 7
TILES = -(-N // P)
GROUPS = TILES // G
PARTS = ((0, 4), (4, G))
PAIRS = [(s, min(s + 2, G)) for s in range(0, G, 2)]
NP = len(PAIRS)
LAST = N - (TILES - 1) * P
CAP = (TILES + 1) * P
NT = 204
SPARE = NT - 2 * N // P
TABLE = NT + 4
SLOTS = E * CAP + SPARE * P
META = 4
ROW = D + META
OUT_ROWS = N + P
SB = 4
PIECES = E * KD
ZB = 4


def wait_from(engine, sem, value):
    if not isinstance(value, int) or value > 0:
        engine.wait_ge(sem, value)


def used(g, q):
    return NP * g + max(q - 1, 0)


def wait_apart(engine, sem, value, apart):
    engine.wait_ge(sem, value)
    engine.sem_inc(apart, 1)


X_STEPS = 26
STATS_STEPS = 26
ROUTE_STEPS = 16
PLACE_STEPS = 10


def experts(nc, engine, tile_expert, i):
    _, numbers = nc.values_load_multi_w_load_instructions(
        tile_expert[0:1, bass.ds(4 * i, 8)], engines=(engine.engine,), min_val=0, max_val=E - 1,
        skip_runtime_bounds_check_because="the table is cut off at the last expert")
    return numbers


class Steps:

    def __init__(self, engine, sem, start):
        self.engine, self.sem, self.start, self.n = engine, sem, start, 0

    def did(self, ins):
        ins.then_inc(self.sem, 1)
        self.n += 1

    def wait(self, apart=None):
        self.engine.wait_ge(self.sem, self.start + self.n)
        if apart is not None:
            self.engine.sem_inc(apart, 1)

    def then(self, ins):
        self.did(ins)
        self.wait()


def build(nc, x, src, dst, edge_weight, gamma, beta, Wr, br, W1, b1, W2, b2, out):
    ctx = ExitStack()
    with ctx:
        def sb(name, shape, dt):
            return ctx.enter_context(nc.sbuf_tensor(name, shape, dt))

        def sem(name):
            return ctx.enter_context(nc.semaphore(name))

        slots = nc.dram_tensor("slots", [SLOTS, ROW], F32, kind="Internal").ap()
        b1_dram = nc.dram_tensor("b1_dram", [E, H], F32, kind="Internal").ap()

        w1h = sb("w1h", [P, E, KD, H], F32R)
        w1l = sb("w1l", [P, E, KD, H], F32R)
        w2h = sb("w2h", [P, E, KH, D], F32R)
        w2l = sb("w2l", [P, E, KH, D], F32R)
        XG = G * D
        arena_x = sb("arena_x", [P, 3 * XG], F32)
        arena_z = sb("arena_z", [P, 2 * G * ROW], F32)
        stage_more = sb("stage_more", [P, H], F32)
        xg = [arena_x[:, b * XG:(b + 1) * XG].rearrange("p (s d) -> p s d", s=G) for b in range(2)]
        xn = arena_x[:, 2 * XG:3 * XG].rearrange("p (s d) -> p s d", s=G)
        stage = [arena_z[:, i * H:(i + 1) * H] for i in range(3)] + [stage_more[:, :]]
        scaled = [arena_z[:, 3 * H:4 * H], arena_x[:, 2 * XG + 4 * D:2 * XG + 4 * D + H]]
        betb = arena_z[:, 4 * H:4 * H + KD * P].rearrange("p (k m) -> p k m", k=KD)
        table_id = arena_x[:, XG:XG + KD * D].rearrange("p (k d) -> p k d", k=KD)
        newer = arena_x[:, XG + KD * D:XG + 2 * KD * D].bitcast(I32).rearrange("p (k d) -> p k d", k=KD)
        hot_s = [arena_x[:, XG + (4 + i) * D:XG + (5 + i) * D] for i in range(2)]
        later = [arena_x[:, XG + 6 * D + i * P:XG + 6 * D + (i + 1) * P] for i in range(2)]
        hot_d = [arena_x[:, 2 * XG + 2 * i * D:2 * XG + 2 * (i + 1) * D].rearrange("p (a d) -> p a d", a=2) for i in range(2)]
        ECT = EBLK * EROWS
        place_raw = arena_z[0:EROWS, 0:ECOLS].bitcast(I32)
        diag_key = arena_z[:, 5 * H:5 * H + PICK * P].rearrange("p (j n) -> p j n", j=PICK)
        zg = [arena_z[:, b * G * ROW:(b + 1) * G * ROW].rearrange("p (s d) -> p s d", s=G) for b in range(2)]
        arena_s = sb("arena_s", [P, 2 * ECT], F32)
        score = arena_s[:, 0:ECT]
        junk = arena_s[:, ECT:2 * ECT]
        raw = [arena_x[0:EROWS, 0:ECOLS], arena_x[0:EROWS, ECOLS:2 * ECOLS]]
        key_raw = raw[0]
        diag_no = junk[:, 0:PICK * P].rearrange("p (j n) -> p j n", j=PICK)
        xT = [arena_s[:, 2 * i * D:2 * (i + 1) * D] for i in range(2)]
        zT = [arena_s[:, 4 * D:6 * D], stage_more[:, :]]
        x1g = arena_s[:, 6 * D:6 * D + XG].rearrange("p (s d) -> p s d", s=G)
        tile_row = arena_s[:, 0:TABLE]
        tmp_t = arena_s[:, TABLE:2 * TABLE]
        zin = [arena_s[:, 4 * D + i * ROW:4 * D + (i + 1) * ROW] for i in range(ZB)]
        EO = 4 * D + ZB * ROW
        ysb = [arena_s[:, EO + i * D:EO + (i + 1) * D] for i in range(2)]
        b1all = arena_x[:, 0:E * H].rearrange("p (e h) -> p e h", e=E)
        b2all = arena_z[:, 0:E * D].rearrange("p (e d) -> p e d", e=E)
        hact = [arena_z[:, E * D + i * H:E * D + (i + 1) * H] for i in range(2)]
        ysum = [arena_z[:, E * D + 2 * H + i * D:E * D + 2 * H + (i + 1) * D] for i in range(2)]

        table = sb("table", [P, KD, D], F32)
        ident = sb("ident", [P, P], F32)
        ones = sb("ones", [P, P], F32)
        onesb = sb("onesb", [P, P], BF16)
        before = sb("before", [P, P], BF16)
        iota_d = sb("iota_d", [P, D], F32)
        iota_e = sb("iota_e", [P, E], F32)
        first_e = sb("first_e", [P, E], F32)
        base_e = sb("base_e", [P, E], F32)
        tok = sb("tok", [P, G], F32)
        gam = sb("gam", [P, KD], F32)
        bet = sb("bet", [P, KD], F32)
        wr = sb("wr", [P, KD, E], F32)
        wrg = sb("wrg", [P, KD, E], F32)
        brb = sb("brb", [P, E], F32)
        lbias = sb("lbias", [P, E], F32)
        bet_e = sb("bet_e", [P, KD, E, E], F32)
        b1row = sb("b1row", [E, H], F32)

        top = sb("top", [P, PICK], F32)
        pkey = sb("pkey", [P, PICK], F32)
        pw = sb("pw", [P, PICK], F32)
        valid = sb("valid", [P, PICK], F32)
        tkey = sb("tkey", [P, PICK], I32)
        trow = sb("trow", [P, PICK], I32)
        tblock = sb("tblock", [P, PICK], I32)
        number = sb("number", [P, PICK], F32)
        first_no = sb("first_no", [P, 1], F32)
        pki = sb("pki", [P, PICK], I32)
        psi = sb("psi", [P, PICK], I32)
        pdi = sb("pdi", [P, PICK], I32)
        psf = sb("psf", [P, PICK], F32)
        pdf = sb("pdf", [P, PICK], F32)
        wanted = sb("wanted", [P, PICK], U32)
        beaten = sb("beaten", [P, PICK], F32)
        alive = sb("alive", [P, PICK], F32)
        first_gelu = sb("first_gelu", [P, 1], F32)
        n_edge = sb("n_edge", [P, 1], F32)
        n_maxf = sb("n_maxf", [1, 1], F32)
        n_max = sb("n_max", [1, 1], I32)

        bn6 = sb("bn6", [P, 2, G, 6], F32)
        mv = sb("mv", [P, 2, G, 2], F32)
        var_u = sb("var_u", [P, 2, G], F32)
        rs_a = sb("rs_a", [P, 2, G], F32)
        rs = sb("rs", [P, 2, G], F32)
        shift = sb("shift", [P, 2, G], F32)
        lg = sb("lg", [P, G, E], F32)
        lg2 = sb("lg2", [P, G, E], F32)
        tmp8 = sb("tmp8", [P, G, E], F32)
        tmp8b = sb("tmp8b", [P, G, E], F32)
        oh = sb("oh", [P, 2, G, E], F32)
        best = sb("best", [P, 2, G], F32)
        which = sb("which", [P, 2, G], F32)
        chosen = sb("chosen", [P, E, G + 1], BF16)
        earlier = sb("earlier", [P, E, G + 1], BF16)
        running = sb("running", [P, E, G + 1], BF16)
        rowok = sb("rowok", [P, 1], F32)
        rank = sb("rank", [P, G, E], F32)
        gap = sb("gap", [P, G], F32)
        egap = sb("egap", [P, G], F32)
        esum = sb("esum", [P, G], F32)
        wtop = sb("wtop", [P, G], F32)
        wsec = sb("wsec", [P, G], F32)
        pos = [sb(f"pos{i}", [P, 2, G], U32) for i in range(2)]

        cnt = sb("cnt", [P, E], F32)
        cnt_i = sb("cnt_i", [P, E], I32)
        tiles_i = sb("tiles_i", [P, E], I32)
        tiles_f = sb("tiles_f", [P, E], F32)
        ends = sb("ends", [P, E], F32)
        jump = sb("jump", [P, E], F32)
        tile_e = sb("tile_e", [P, TABLE], F32)
        tile_i = sb("tile_i", [1, 2, TABLE], I32)
        tail_i = sb("tail_i", [1, E], I32)
        filler = sb("filler", [P, ROW], F32)

        xh = [sb(f"xh{i}", [P, D], F32R) for i in range(2)]
        xl = [sb(f"xl{i}", [P, D], F32R) for i in range(2)]
        hh = [sb(f"hh{i}", [P, H], F32R) for i in range(2)]
        hl = sb("hl", [P, H], F32R)
        second = [sb(f"second{i}", [P, 1], F32) for i in range(ZB)]
        ywt = [sb(f"ywt{i}", [P, 1], F32) for i in range(ZB)]
        yid = [sb(f"yid{i}", [P, 1], U32) for i in range(ZB)]

        psum = ctx.enter_context(nc.psum_tensor("psum", [P, 8, 512], F32))
        bank = [psum[:, i, :] for i in range(8)]

        s_const = sem("s_const")
        dve_passed = sem("dve_passed")
        pool_passed = sem("pool_passed")
        raw_in = sem("raw_in")
        small_in = sem("small_in")
        keys_ready = sem("keys_ready")
        score_zeroed = sem("score_zeroed")
        block_turned = sem("block_turned")
        block_out = sem("block_out")
        edge_step = sem("edge_step")
        n_edge_ready = sem("n_edge_ready")
        n_edge_turned = sem("n_edge_turned")
        n_max_ready = sem("n_max_ready")
        wanted_ready = sem("wanted_ready")
        weights_in = sem("weights_in")
        diag_ready = sem("diag_ready")
        rows_ready = sem("rows_ready")
        hot_ready = sem("hot_ready")
        new_ready = sem("new_ready")
        table_ready = sem("table_ready")

        stage_in = [sem(f"stage_in{i}") for i in range(SB)]
        w_high = sem("w_high")
        w_product = sem("w_product")
        w_low = sem("w_low")
        w_read = sem("w_read")
        bias_added = sem("bias_added")
        bias_out = sem("bias_out")
        b1_in = sem("b1_in")
        b2_in = sem("b2_in")
        lbias_mm = sem("lbias_mm")
        lbias_ready = sem("lbias_ready")
        wrg_ready = sem("wrg_ready")
        scratch_ready = sem("scratch_ready")

        x_in = [[sem(f"x_in{i}_{h}") for h in range(2)] for i in range(2)]
        x1_out = [sem(f"x1_out{h}") for h in range(2)]
        stats_step = sem("stats_step")
        x_step = sem("x_step")
        x_scale_ready = sem("x_scale_ready")
        z_scale_ready = sem("z_scale_ready")
        xn_ready = sem("xn_ready")
        xT_mm = sem("xT_mm")
        xT_ready = sem("xT_ready")
        g_ready = sem("g_ready")
        g_added = sem("g_added")
        z_ready = sem("z_ready")
        zT_mm = sem("zT_mm")
        zT_ready = sem("zT_ready")
        logits_ready = sem("logits_ready")
        route_step = sem("route_step")
        place_step = sem("place_step")
        gap_ready = sem("gap_ready")
        egap_ready = sem("egap_ready")
        chosen_ready = sem("chosen_ready")
        rank_ready = sem("rank_ready")
        routed = sem("routed")
        sent = [sem(f"sent{i}") for i in range(2)]

        count_mm = sem("count_mm")
        count_step = sem("count_step")
        tables_ready = sem("tables_ready")
        filled = sem("filled")

        z_in = [sem(f"z_in{i}") for i in range(ZB)]
        zx_mm = sem("zx_mm")
        xh_ready = sem("xh_ready")
        xl_ready = sem("xl_ready")
        meta_step = sem("meta_step")
        meta_ready = sem("meta_ready")
        h_mm = sem("h_mm")
        h_added = sem("h_added")
        h_ready = sem("h_ready")
        hT_mm = sem("hT_mm")
        hh_ready = sem("hh_ready")
        hl_ready = sem("hl_ready")
        y_mm = sem("y_mm")
        y_added = sem("y_added")
        y_ready = [sem(f"y_ready{i}") for i in range(2)]
        y_out = [sem(f"y_out{i}") for i in range(2)]

        x_tiled = x[0:(TILES - 1) * P, :].rearrange("(n p) d -> p n d", p=P)
        out_tiled = out[0:(TILES - 1) * P, :].rearrange("(n p) d -> p n d", p=P)

        block = ctx.enter_context(nc.Block())

        @block.sync
        def _(sp):
            for i, a in enumerate((src, dst)):
                sp.dma_start(raw[i].bitcast(a.dtype), a.rearrange("(p c) -> p c", p=EROWS)).then_inc(raw_in, 16)
            sp.dma_start(wr[:, :, :], Wr.rearrange("(k p) e -> p k e", p=P)).then_inc(small_in, 16)
            with nc.allow_non_contiguous_dma(reason="two values a partition"):
                sp.dma_start(gam[:, :], gamma.rearrange("(k p) -> p k", p=P)).then_inc(small_in, 16)
                sp.dma_start(bet[:, :], beta.rearrange("(k p) -> p k", p=P)).then_inc(small_in, 16)
            sp.dma_start(brb[:, :], br.rearrange("(a e) -> a e", a=1).to_broadcast([P, E])).then_inc(small_in, 16)
            sp.dma_start(b1row[:, :], b1).then_inc(small_in, 16)
            sp.wait_ge(block_turned, EBLK)

            def load_x(g, b, h, full=True):
                lo, hi = PARTS[h]
                if full or h == 0:
                    sp.dma_start(xg[b][:, lo:hi, :], x_tiled[:, bass.ds(g * G + lo, hi - lo), :]).then_inc(x_in[b][h], 16)
                else:
                    sp.dma_start(xg[b][:, lo:hi - 1, :], x_tiled[:, g * G + lo:g * G + hi - 1, :]).then_inc(x_in[b][h], 16)
                    sp.dma_start(xg[b][0:LAST, G - 1, :], x[(TILES - 1) * P:N, :]).then_inc(x_in[b][h], 16)

            def turn_over(g, b, load=True, full=True):
                for h, (lo, hi) in enumerate(PARTS):
                    sp.wait_ge(g_added, NP * g + (hi + 1) // 2)
                    sp.dma_start(out_tiled[:, bass.ds(g * G + lo, hi - lo), :], x1g[:, lo:hi, :]).then_inc(x1_out[h], 16)
                    if load:
                        load_x(g + 2, b, h, full)

            w1_pieces = W1.rearrange("(i u) (k p) h -> i u k p h", u=2, p=P)
            w2_pieces = W2.rearrange("(i u) (k p) d -> i u k p d", u=2, p=P)

            def load_w1(i, b):
                before = SB * i + b + 1 - SB
                wait_from(sp, w_read, before)
                wait_from(sp, w_product, before)
                sp.dma_start(stage[b], w1_pieces[bass.ds(i, 1), b // 2, b % 2, :, :].rearrange("a p h -> p (a h)")).then_inc(stage_in[b], 16)
            for b in range(SB):
                load_w1(0, b)
            for h in range(2):
                load_x(0, 0, h)
            with sp.Fori(1, E // 2) as i:
                for b in range(SB):
                    load_w1(i, b)

            def load_w2(i, b):
                sp.dma_start(stage[b].rearrange("p (k d) -> p k d", k=2),
                             w2_pieces[bass.ds(i, 1), b // 2, 2 * (b % 2):2 * (b % 2) + 2, :, :].rearrange("a k p d -> p (a k) d")).then_inc(stage_in[b], 16)
            for b in range(SB):
                sp.wait_ge(w_read, PIECES - SB + b + 1)
                sp.wait_ge(w_product, PIECES - SB + b + 1)
                load_w2(0, b)
            def more_w2(lo, hi):
                with sp.Fori(lo, hi) as i:
                    for b in range(SB):
                        sp.wait_ge(w_low, PIECES + SB * (i - 1) + b + 1)
                        load_w2(i, b)
            more_w2(1, HALF)

            sp.wait_ge(table_ready, 1)
            for h in range(2):
                load_x(1, 1, h)
            more_w2(HALF, E // 2)
            sp.wait_ge(bias_added, 1)
            sp.dma_start(b1_dram, b1row[:, :]).then_inc(bias_out, 16)
            with sp.Fori(0, GROUPS // 2 - 2) as i:
                for u in range(2):
                    turn_over(2 * i + u, u)
            turn_over(GROUPS - 4, 0)
            turn_over(GROUPS - 3, 1, full=False)
            turn_over(GROUPS - 2, 0, load=False)
            lo, hi = PARTS[1]
            sp.wait_ge(g_added, NP * GROUPS)
            sp.dma_start(out_tiled[:, (GROUPS - 1) * G:(GROUPS - 1) * G + lo, :], x1g[:, 0:lo, :]).then_inc(x1_out[0], 16)
            sp.dma_start(out_tiled[:, (GROUPS - 1) * G + lo:TILES - 1, :], x1g[:, lo:G - 1, :]).then_inc(x1_out[1], 16)
            sp.dma_start(out[(TILES - 1) * P:N, :], x1g[0:LAST, G - 1, :]).then_inc(x1_out[1], 16)

            sp.wait_ge(s_const, 4)
            sp.dma_start(out[N:OUT_ROWS, :], filler[:, 0:D]).then_inc(filled, 16)
            sp.dma_start(slots[E * CAP:SLOTS, :].rearrange("(n p) d -> p n d", p=P),
                         filler[:, :].unsqueeze(1).to_broadcast([P, SPARE, ROW])).then_inc(filled, 16)
            sp.wait_ge(tables_ready, 1)
            for e in range(E):
                r = sp.value_load(tail_i[0:1, e:e + 1], min_val=0, max_val=E * CAP)
                sp.dma_start(slots[bass.ds(r, P), :], filler[:, :]).then_inc(filled, 16)
            for b in range(2):
                for h in range(2):
                    sp.wait_ge(x_in[b][h], 16 * GROUPS // 2 + 16 * (b + h == 2))
            sp.wait_ge(bias_out, 16)
            sp.dma_start(b1all, b1_dram.rearrange("(a e) h -> a e h", a=1).to_broadcast([P, E, H])).then_inc(b1_in, 16)
            sp.wait_ge(filled, 16 * (E + 2))
            for b in range(2):
                sp.wait_ge(sent[b], 16 * 2 * G * GROUPS // 2)

            def load_z(i, u):
                r = sp.value_load(tile_i[0:1, 1, bass.ds(4 * i + u, 1)], min_val=0, max_val=SLOTS - P)
                sp.dma_start(zin[u % ZB][:, :], slots[bass.ds(r, P), :]).then_inc(z_in[u % ZB], 16)

            for h in range(2):
                sp.wait_ge(x1_out[h], 16 * (GROUPS + h))
            for u in range(ZB):
                load_z(0, u)
            sp.dma_start(b2all, b2.rearrange("(a e) d -> a e d", a=1).to_broadcast([P, E, D])).then_inc(b2_in, 16)
            with sp.Fori(1, NT // ZB) as i:
                for u in range(ZB):
                    sp.wait_ge(zx_mm, ZB * i + u - 3)
                    sp.wait_ge(meta_ready, ZB * i + u - 3)
                    load_z(i, u)

        @block.gpsimd
        def _(pool):
            for i in range(EBLK):
                lo, hi = i * P, min((i + 1) * P, ECOLS)
                pool.iota(place_raw[:, lo:hi], pattern=[[0, hi - lo]], base=(ROW0 << 20) + (i << 16), channel_multiplier=1 << 20)
            pool.memset(filler[:, 0:D], 0.0)
            pool.memset(filler[:, D + 1:ROW], 0.0).then_inc(s_const, 1)
            pool.iota(filler[:, D:D + 1], pattern=[[0, 1]], base=N, channel_multiplier=1, allow_small_or_imprecise_dtypes=True)
            pool.memset(ident[:, :], 0.0).then_inc(s_const, 1)
            pool.memset(onesb[:, :], 1.0)
            pool.memset(before[:, :], 1.0).then_inc(s_const, 1)
            pool.wait_ge(s_const, 3)
            pool.affine_select(out=ident[:, :], in_=ident[:, :], compare_op=ALU.not_equal, fill=1.0,
                               base=0, pattern=[[-1, P]], channel_multiplier=1)
            pool.affine_select(out=before[:, :], in_=before[:, :], compare_op=ALU.is_gt, fill=0.0,
                               base=0, pattern=[[1, P]], channel_multiplier=-1)
            pool.memset(ones[:, :], 1.0)
            pool.memset(table[:, :, :], 0.0)
            pool.memset(bet_e[:, :, :, :], 0.0)
            pool.iota(first_no[:, :], pattern=[[0, 1]], base=1 - ROW0 * ECOLS, channel_multiplier=1, allow_small_or_imprecise_dtypes=True)
            pool.memset(score, 0.0).then_inc(score_zeroed, 1)
            pool.memset(running[:, :, 1:G + 1], 1.0)
            pool.memset(running[:, :, 0:1], 0.0)
            pool.memset(chosen[:, :, 0:1], 0.0)
            pool.memset(tile_e[:, :], 0.0)
            pool.iota(iota_d[:, :], pattern=[[1, D]], base=0, channel_multiplier=0, allow_small_or_imprecise_dtypes=True)
            pool.iota(iota_e[:, :], pattern=[[1, E]], base=0, channel_multiplier=0, allow_small_or_imprecise_dtypes=True)
            pool.iota(first_e[:, :], pattern=[[-1, E]], base=E, channel_multiplier=0, allow_small_or_imprecise_dtypes=True)
            pool.iota(base_e[:, :], pattern=[[CAP, E]], base=0, channel_multiplier=0, allow_small_or_imprecise_dtypes=True)
            pool.iota(rowok[:, :], pattern=[[0, 1]], base=0, channel_multiplier=1, allow_small_or_imprecise_dtypes=True)
            pool.iota(tok[:, :], pattern=[[P, G]], base=0, channel_multiplier=1, allow_small_or_imprecise_dtypes=True).then_inc(s_const, 1)
            def low(ready, c, target, full, high):
                wait_apart(pool, ready, c, pool_passed)
                pool.tensor_tensor(target, full, high, ALU.subtract).then_inc(w_low, 1)

            pool.wait_ge(block_turned, EBLK)
            pool.memset(table_id[:, :, :], 0.0).then_inc(scratch_ready, 1)

            def fetch(r):
                wait_apart(pool, wanted_ready, r + 1, pool_passed)
                for j in range(PICK):
                    pool.indirect_dma_start(pw[:, j:j + 1], None, edge_weight.rearrange("(n a) -> n a", a=1),
                                            bass.IndirectOffsetOnAxis(ap=wanted[:, j:j + 1], axis=0)).then_inc(weights_in, 16)
            fetch(0)
            with pool.Fori(0, E) as e:
                for k in range(KD):
                    wait_apart(pool, w_high, 2 * e + k + 1, pool_passed)
                    low(w_product, 2 * e + k + 1, w1l[:, bass.ds(e, 1), k, :].rearrange("p a h -> p (a h)"), scaled[k],
                        w1h[:, bass.ds(e, 1), k, :].rearrange("p a h -> p (a h)").bitcast(F32))
            def low2(lo, hi):
                with pool.Fori(lo, hi) as i:
                    for b in range(SB):
                        e, k = 2 * i + b // 2, b % 2
                        low(w_high, PIECES + SB * i + b + 1, w2l[:, bass.ds(e, 1), 2 * k:2 * k + 2, :].rearrange("p a k d -> p (a k d)"), stage[b],
                            w2h[:, bass.ds(e, 1), 2 * k:2 * k + 2, :].rearrange("p a k d -> p (a k d)").bitcast(F32))
            low2(0, HALF)
            pool.wait_ge(n_max_ready, 1)
            most = pool.value_load(n_max[0:1, 0:1], min_val=0, max_val=ECT)
            with pool.If(most > PICK):
                with pool.Fori(1, ROUNDS) as r:
                    with pool.If(most > PICK * r):
                        fetch(r)
            low2(HALF, E // 2)
            def send(g, b, full=True):
                wait_apart(pool, routed, g + 1, pool_passed)
                for s in range(G):
                    n = P if full or s < G - 1 else LAST
                    for k in range(2):
                        pool.indirect_dma_start(slots[:, :], bass.IndirectOffsetOnAxis(ap=pos[b][0:n, k, s:s + 1], axis=0),
                                                zg[b][0:n, s, :], None).then_inc(sent[b], 16)
            with pool.Fori(0, GROUPS // 2 - 1) as i:
                for u in range(2):
                    send(2 * i + u, u)
            send(GROUPS - 2, 0)
            send(GROUPS - 1, 1, full=False)
            def scatter_add(i, u):
                b = u % 2
                wait_apart(pool, y_ready[b], 2 * i + u // 2 + 1, pool_passed)
                before = 32 * i + 16 * ((u + 1) // 2)
                if isinstance(i, int):
                    wait_from(pool, y_out[1 - b], before)
                else:
                    wait_apart(pool, y_out[1 - b], before, pool_passed)
                pool.indirect_dma_start(out[:, :], bass.IndirectOffsetOnAxis(ap=yid[u][:, 0:1], axis=0),
                                        ysb[b][:, :], None, compute_op=ALU.add).then_inc(y_out[b], 16)
            for h in range(2):
                pool.wait_ge(x1_out[h], 16 * (GROUPS + h))
            pool.wait_ge(filled, 16 * (E + 2))
            for u in range(ZB):
                scatter_add(0, u)
            with pool.Fori(1, NT // ZB) as i:
                for u in range(ZB):
                    scatter_add(i, u)
            for u in range(2):
                pool.wait_ge(y_out[u], 16 * NT // 2)

        @block.tensor
        def _(pe):
            def wide(b, n):
                return bank[b][:, 0:n]

            pe.wait_ge(s_const, 4)
            pe.wait_ge(keys_ready, 1)
            for i in range(EBLK):
                m = P if i < EBLK - 1 else ELAST
                nc.tensor.transpose(bank[i // 4][0:m, (i % 4) * P:(i % 4) * P + EROWS],
                                    key_raw[:, i * P:i * P + m], ident[0:EROWS, 0:EROWS]).then_inc(block_turned, 1)
            pe.wait_ge(block_out, 4)
            pe.wait_ge(n_edge_ready, 1)
            nc.tensor.transpose(bank[5][0:1, 0:P], n_edge[:, :], ident[:, :]).then_inc(n_edge_turned, 1)
            pe.wait_ge(wrg_ready, 1)
            for k in range(KD):
                last = nc.tensor.matmul(bank[6][:, 0:E], betb[:, k, :], wr[:, k, :], start=(k == 0), stop=(k == KD - 1))
            last.then_inc(lbias_mm, 1)

            def bias_product(e):
                for k in range(KD):
                    n = KD * e + k
                    pe.wait_ge(stage_in[n % SB], 16 * (n // SB) + 16)
                    nc.tensor.matmul(bank[7][0:E, :], bet_e[:, k, e, :], stage[n % SB], start=(n == 0), stop=(n == PIECES - 1)).then_inc(w_read, 1)
            for e in range(EARLY):
                bias_product(e)
            pe.wait_ge(n_max_ready, 1)
            most = pe.value_load(n_max[0:1, 0:1], min_val=0, max_val=ECT)

            def picks(r, late=()):
                pe.wait_ge(diag_ready, r + 1)
                for q in range(2):
                    nc.tensor.matmul(bank[q], ones[:, :], diag_key[:, 4 * q:4 * q + 4, :].rearrange("p j n -> p (j n)"), start=True, stop=True)
                    last = nc.tensor.matmul(bank[2 + q], ones[:, :], diag_no[:, 4 * q:4 * q + 4, :].rearrange("p j n -> p (j n)"), start=True, stop=True)
                last.then_inc(rows_ready, 1)
                for j in range(PICK):
                    if j < len(late):
                        bias_product(late[j])
                    pe.wait_ge(hot_ready, PICK * r + j + 1)
                    for m in range(KD):
                        last = nc.tensor.matmul(bank[4 * (1 - j % 2) + m], hot_s[j % 2][:, m * P:(m + 1) * P],
                                                hot_d[j % 2].rearrange("p a n -> p (a n)"), start=True, stop=True)
                    last.then_inc(new_ready, 1)
            picks(0, late=range(EARLY, E))
            with pe.If(most > PICK):
                with pe.Fori(1, ROUNDS) as r:
                    with pe.If(most > PICK * r):
                        picks(r)

            def turn(pair, source, target):
                for a, s in enumerate(range(*pair)):
                    for k in range(KD):
                        last = nc.tensor.transpose(target[:, a * D + k * P:a * D + (k + 1) * P], source[:, s, k * P:(k + 1) * P], ident[:, :])
                return last

            def turn_x(g, q):
                pe.wait_ge(xn_ready, G * g + PAIRS[q][1])
                turn(PAIRS[q], xn, bank[q % 2]).then_inc(xT_mm, 1)

            def edge_product(g, q):
                pe.wait_ge(xT_ready, NP * g + q + 1)
                wait_from(pe, g_added, used(g, q))
                for a in range(PAIRS[q][1] - PAIRS[q][0]):
                    for k in range(KD):
                        last = nc.tensor.matmul(bank[2 + q % 2][:, a * D:(a + 1) * D], xT[q % 2][:, a * D + k * P:a * D + (k + 1) * P], table[:, k, :],
                                                start=(k == 0), stop=(k == KD - 1))
                last.then_inc(g_ready, 1)

            def turn_z(g, q, b):
                pe.wait_ge(z_ready, G * g + PAIRS[q][1])
                turn(PAIRS[q], zg[b], bank[4 + q % 2]).then_inc(zT_mm, 1)

            def logits(g, q):
                pe.wait_ge(zT_ready, NP * g + q + 1)
                for a, s in enumerate(range(*PAIRS[q])):
                    for k in range(KD):
                        last = nc.tensor.matmul(bank[6][:, s * E:(s + 1) * E], zT[q % 2][:, a * D + k * P:a * D + (k + 1) * P], wrg[:, k, :],
                                                start=(k == 0), stop=(k == KD - 1))
                last.then_inc(logits_ready, 1)

            def ranks(g):
                pe.wait_ge(chosen_ready, g + 1)
                o = bank[7][:, 0:G * E].rearrange("p (e s) -> p e s", e=E)
                nc.tensor.matmul(o, before[:, :], chosen[:, :, 1:G + 1], start=True, stop=False)
                nc.tensor.matmul(o, onesb[:, :], earlier[:, :, 0:G],
                                 start=False, stop=True).then_inc(rank_ready, 1)

            def group(g, b, x_side=True, z_side=True, older=True):
                if x_side:
                    turn_x(g, 0)
                    turn_x(g, 1)
                    edge_product(g, 0)
                    turn_x(g, 2)
                    turn_x(g, 3)
                if older:
                    ranks(g - 2)
                if x_side:
                    edge_product(g, 1)
                if z_side:
                    turn_z(g - 1, 0, 1 - b)
                    turn_z(g - 1, 1, 1 - b)
                    logits(g - 1, 0)
                for q in range(2, NP):
                    if x_side:
                        edge_product(g, q)
                    if z_side:
                        turn_z(g - 1, q, 1 - b)
                        logits(g - 1, q - 1)
                if z_side:
                    logits(g - 1, NP - 1)

            group(0, 0, z_side=False, older=False)
            group(1, 1, older=False)
            with pe.Fori(1, GROUPS // 2) as i:
                for u in range(2):
                    group(2 * i + u, u)
            group(GROUPS, 0, x_side=False)
            ranks(GROUPS - 1)
            pe.wait_ge(routed, GROUPS)
            nc.tensor.matmul(bank[6][:, 0:E], onesb[:, :], earlier[:, :, G], start=True, stop=True).then_inc(count_mm, 1)

            pe.wait_ge(tables_ready, 1)
            pe.wait_ge(w_low, 2 * PIECES)

            def turn_z(i, u):
                pe.wait_ge(z_in[u % ZB], 16 * (i + u // ZB) + 16)
                wait_from(pe, xl_ready, 4 * i + u - 1)
                for k in range(KD):
                    last = nc.tensor.transpose(bank[u % 2][:, k * P:(k + 1) * P], zin[u % ZB][:, k * P:(k + 1) * P], ident[:, :])
                last.then_inc(zx_mm, 1)

            def up(i, u, e):
                j, b = 4 * i + u, u % 2
                pe.wait_ge(xl_ready, j + 1)
                wait_from(pe, h_added, j - 1)
                for k in range(KD):
                    for xs, ws in ((xh, w1h), (xh, w1l), (xl, w1h)):
                        last = nc.tensor.matmul(bank[2 + b], xs[b][:, k * P:(k + 1) * P], ws[:, bass.ds(e, 1), k, :].rearrange("p a h -> p (a h)"),
                                                start=(k == 0 and ws is w1h and xs is xh), stop=(k == KD - 1 and xs is xl))
                last.then_inc(h_mm, 1)

            def turn_h(i, u):
                j, b = 4 * i + u, u % 2
                pe.wait_ge(h_ready, j + 1)
                wait_from(pe, hl_ready, j - 1)
                for k in range(KH):
                    last = nc.tensor.transpose(bank[4 + b][:, k * P:(k + 1) * P], hact[b][:, k * P:(k + 1) * P], ident[:, :])
                last.then_inc(hT_mm, 1)

            def down(i, u, e):
                j, b = 4 * i + u, u % 2
                pe.wait_ge(hl_ready, j + 1)
                wait_from(pe, y_added, j - 1)
                for k in range(KH):
                    for hs, ws in ((hh[b], w2h), (hh[b], w2l), (hl, w2h)):
                        last = nc.tensor.matmul(bank[6 + b][:, 0:D], hs[:, k * P:(k + 1) * P], ws[:, bass.ds(e, 1), k, :].rearrange("p a h -> p (a h)"),
                                                start=(k == 0 and ws is w2h and hs is not hl), stop=(k == KH - 1 and hs is hl))
                last.then_inc(y_mm, 1)

            def tile_step(i, u, es, left=4):
                if left > 3:
                    turn_z(i, u + 3)
                if left > 2:
                    up(i, u + 2, es[u + 2])
                if left > 1:
                    turn_h(i, u + 1)
                down(i, u, es[u])

            es = experts(nc, pe, tile_i[:, 0, :], 0)
            for u in range(3):
                turn_z(0, u)
                if u < 2:
                    up(0, u, es[u])
            turn_h(0, 0)
            for u in range(4):
                tile_step(0, u, es)
            with pe.Fori(1, NT // 4 - 1) as i:
                es = experts(nc, pe, tile_i[:, 0, :], i)
                for u in range(4):
                    tile_step(i, u, es)
            es = experts(nc, pe, tile_i[:, 0, :], NT // 4 - 1)
            for u in range(4):
                tile_step(NT // 4 - 1, u, es, 4 - u)

        @block.vector
        def _(dve):
            v = nc.vector
            dve.wait_ge(raw_in, 32)
            t = Steps(dve, edge_step, 0)
            outer = junk[0:EROWS, 0:ECOLS]
            src_i, dst_i = raw[0].bitcast(I32), raw[1].bitcast(I32)
            t.did(v.tensor_tensor(outer, src_i, dst_i, ALU.max))
            t.then(v.scalar_tensor_tensor(out=src_i, in0=src_i, scalar=8, in1=dst_i, op0=ALU.logical_shift_left, op1=ALU.bitwise_or))
            dve.wait_ge(s_const, 1)
            t.then(v.tensor_tensor(src_i, src_i, place_raw, ALU.bitwise_or))
            v.scalar_tensor_tensor(out=key_raw, in0=outer, scalar=float(D), in1=key_raw, op0=ALU.is_lt, op1=ALU.mult).then_inc(keys_ready, 1)
            dve.wait_ge(block_out, 4)
            dve.wait_ge(s_const, 4)
            dve.wait_ge(scratch_ready, 1)
            dve.wait_ge(small_in, 80)
            for k in range(KD):
                v.tensor_scalar(wrg[:, k, :], wr[:, k, :], gam[:, k:k + 1], None, ALU.mult)
                v.tensor_copy(bet_e[:, k, :, :].rearrange("p a b -> p (a b)")[:, 0:E * E:E + 1], bet[:, k:k + 1].to_broadcast([P, E]))
                last = v.tensor_scalar(betb[:, k, :], ones[:, :], bet[:, k:k + 1], None, ALU.mult)
            last.then_inc(wrg_ready, 1)
            v.tensor_scalar(junk, score, 0.0, None, ALU.is_gt, ALU.add, accum_out=n_edge[:, :]).then_inc(n_edge_ready, 1)
            dve.wait_ge(n_edge_turned, 1)
            t.then(v.tensor_reduce(n_maxf[:, :], bank[5][0:1, 0:P], AX.X, ALU.max))
            v.tensor_copy(n_max[:, :], n_maxf[:, :]).then_inc(n_max_ready, 1)
            dve.wait_ge(n_max_ready, 1)
            most = dve.value_load(n_max[0:1, 0:1], min_val=0, max_val=ECT)
            edge_before = t.n

            def over_tiles(a):
                return a.unsqueeze(1).to_broadcast([P, G, E])

            def over_experts(a):
                return a.unsqueeze(2).to_broadcast([P, G, E])

            def rsqrt(t, a):
                u, w, r = var_u[:, a, :], rs_a[:, a, :], rs[:, a, :]
                t.wait()
                t.did(v.tensor_scalar(w.bitcast(I32), u.bitcast(I32), 1, None, ALU.arith_shift_right))
                yield
                t.wait()
                t.did(v.tensor_scalar(r.bitcast(I32), w.bitcast(I32), -1.0, float(0x5f3759df), ALU.mult, ALU.add))
                yield
                for _ in range(3):
                    t.wait()
                    t.did(v.tensor_tensor(w, r, r, ALU.mult))
                    yield
                    t.wait()
                    t.did(v.scalar_tensor_tensor(out=w, in0=w, scalar=-0.5, in1=u, op0=ALU.mult, op1=ALU.mult))
                    yield
                    t.wait()
                    t.did(v.scalar_tensor_tensor(out=r, in0=w, scalar=1.5, in1=r, op0=ALU.add, op1=ALU.mult))
                    yield

            def shifts(a, ready):
                v.scalar_tensor_tensor(out=shift[:, a, :], in0=mv[:, a, :, 0], scalar=-1.0, in1=rs[:, a, :], op0=ALU.mult, op1=ALU.mult).then_inc(ready, 1)

            def x_scales(g, b, loads=1, first=False):
                t = Steps(dve, x_step, X_STEPS * g)
                for s in range(G):
                    for h, (lo, hi) in enumerate(PARTS):
                        if s == lo:
                            dve.wait_ge(x_in[b][h], 8 * (g - b) + 16 * (loads if h == 1 else 1))
                    t.did(v.bn_stats(bn6[:, 1, s, :], xg[b][:, s, :]))
                    yield
                t.wait(apart=dve_passed)
                for s in range(G):
                    t.did(v.bn_aggr(mv[:, 1, s, :], bn6[:, 1, s, :]))
                    yield
                t.wait()
                t.did(v.tensor_scalar(var_u[:, 1, :], mv[:, 1, :, 1], 1.0, EPS, ALU.mult, ALU.add))
                yield
                if not first:
                    dve.wait_ge(xn_ready, G * g)
                for _ in rsqrt(t, 1):
                    yield
                t.wait()
                shifts(1, x_scale_ready)
                assert t.n == X_STEPS, t.n

            def over_columns(a):
                return a.unsqueeze(2).to_broadcast([P, PICK, P])

            def pick_round(r, start, spare=iter(())):
                t = Steps(dve, edge_step, start)
                t.then(v.max(top[:, :], score))
                word = top[:, :].bitcast(I32)
                t.did(v.tensor_scalar(tkey[:, :], word, D * D - 1, None, ALU.bitwise_and))
                t.did(v.tensor_scalar(trow[:, :], word, 20, None, ALU.logical_shift_right))
                t.did(v.tensor_scalar(tblock[:, :], word, 9, 15 * P, ALU.logical_shift_right, ALU.bitwise_and))
                t.did(v.tensor_scalar(valid[:, :], top[:, :], 0.0, None, ALU.is_gt))
                t.wait()
                t.did(v.scalar_tensor_tensor(out=pkey[:, :], in0=tkey[:, :], scalar=1.0, in1=valid[:, :], op0=ALU.add, op1=ALU.mult))
                t.then(v.scalar_tensor_tensor(out=number[:, :], in0=trow[:, :], scalar=float(ECOLS), in1=tblock[:, :], op0=ALU.mult, op1=ALU.add))
                t.then(v.scalar_tensor_tensor(out=number[:, :], in0=number[:, :], scalar=first_no[:, :], in1=valid[:, :], op0=ALU.add, op1=ALU.mult))
                v.tensor_scalar(wanted[:, :], number[:, :], 1.0, 0.0, ALU.subtract, ALU.max).then_inc(wanted_ready, 1)
                t.wait(apart=dve_passed)
                t.did(v.tensor_tensor(diag_key, ident[:, :].unsqueeze(1).to_broadcast([P, PICK, P]), over_columns(pkey[:, :]), ALU.mult))
                v.tensor_tensor(diag_no, ident[:, :].unsqueeze(1).to_broadcast([P, PICK, P]), over_columns(number[:, :]), ALU.mult).then_inc(diag_ready, 1)
                t.did(v.match_replace(out=score, in_to_replace=top[:, :], in_values=score, imm_value=0.0))
                t.did(v.tensor_scalar(pki[:, :], pkey[:, :], 1.0, None, ALU.subtract))
                t.wait()
                t.did(v.tensor_scalar(psi[:, :], pki[:, :], 8, None, ALU.arith_shift_right))
                t.did(v.tensor_scalar(pdi[:, :], pki[:, :], D - 1, None, ALU.bitwise_and))
                t.wait()
                t.did(v.tensor_copy(psf[:, :], psi[:, :]))
                t.did(v.tensor_copy(pdf[:, :], pdi[:, :]))
                for _ in range(G):
                    next(spare, None)
                dve.wait_ge(rows_ready, r + 1)
                for j in range(PICK + 1):
                    if j < PICK:
                        t.did(v.tensor_scalar(later[j % 2], bank[2 + j // 4][:, (j % 4) * P:(j % 4 + 1) * P], number[:, j:j + 1], None, ALU.is_gt))
                    if j > 0:
                        a = j - 1
                        t.wait()
                        t.did(v.scalar_tensor_tensor(out=later[a % 2], in0=bank[a // 4][:, (a % 4) * P:(a % 4 + 1) * P], scalar=pkey[:, a:a + 1],
                                                     in1=later[a % 2], op0=ALU.is_equal, op1=ALU.mult, accum_out=beaten[:, a:a + 1]))
                        if j < PICK:
                            t.wait()
                t.wait()
                t.did(v.tensor_scalar(alive[:, :], beaten[:, :], 0.0, None, ALU.is_equal))
                t.wait()
                dve.wait_ge(weights_in, 16 * PICK * r + 16 * PICK)

                def hot(j):
                    v.tensor_scalar(hot_s[j % 2], iota_d[:, :], psf[:, j:j + 1], alive[:, j:j + 1], ALU.is_equal, ALU.mult)
                    v.tensor_scalar(hot_d[j % 2][:, 0, :], iota_d[:, :], pdf[:, j:j + 1], pw[:, j:j + 1], ALU.is_equal, ALU.mult)
                    v.tensor_scalar(hot_d[j % 2][:, 1, :], iota_d[:, :], pdf[:, j:j + 1], number[:, j:j + 1], ALU.is_equal, ALU.mult).then_inc(hot_ready, 1)
                hot(0)
                hot(1)
                for _ in spare:
                    pass
                for j in range(PICK):
                    b = 4 * (1 - j % 2)
                    t.wait(apart=dve_passed)
                    dve.wait_ge(new_ready, PICK * r + j + 1)
                    t.did(v.tensor_tensor(newer[:, :, :], psum[:, b:b + KD, D:2 * D], table_id[:, :, :], ALU.is_gt))
                    t.did(v.tensor_tensor(table_id[:, :, :], psum[:, b:b + KD, D:2 * D], table_id[:, :, :], ALU.max))
                    t.wait(apart=dve_passed)
                    t.did(v.copy_predicated(table[:, :, :], newer[:, :, :], psum[:, b:b + KD, 0:D]))
                    if j + 2 < PICK:
                        hot(j + 2)
                return t.n
            per_round = pick_round(0, edge_before, x_scales(0, 0, first=True))
            with dve.If(most > PICK):
                with dve.Fori(1, ROUNDS) as r:
                    with dve.If(most > PICK * r):
                        pick_round(r, edge_before + per_round * r)
            v.memset(gap[:, :], 0.0).then_inc(table_ready, 1)
            v.tensor_tensor(lbias[:, :], bank[6][:, 0:E], brb[:, :], ALU.add).then_inc(lbias_ready, 1)
            dve.wait_ge(w_read, PIECES)
            v.tensor_tensor(b1row[:, :], bank[7][0:E, :], b1row[:, :], ALU.add).then_inc(bias_added, 1)

            def route(g, b, full=True):
                t = Steps(dve, route_step, ROUTE_STEPS * g)
                dve.wait_ge(logits_ready, NP * g + NP)
                t.did(v.tensor_tensor(lg[:, :, :], bank[6][:, 0:G * E].rearrange("p (s e) -> p s e", s=G), over_tiles(lbias[:, :]), ALU.add))
                yield
                for k, l in ((0, lg), (1, lg2)):
                    t.wait()
                    t.did(v.tensor_reduce(best[:, k, :], l[:, :, :], AX.X, ALU.max))
                    yield
                    t.wait()
                    t.did(v.tensor_tensor(tmp8[:, :, :], l[:, :, :], over_experts(best[:, k, :]), ALU.is_equal))
                    yield
                    t.wait()
                    t.did(v.tensor_tensor(tmp8[:, :, :], tmp8[:, :, :], over_tiles(first_e[:, :]), ALU.mult))
                    yield
                    t.wait()
                    t.did(v.tensor_reduce(which[:, k, :], tmp8[:, :, :], AX.X, ALU.max))
                    yield
                    t.wait()
                    t.did(v.tensor_tensor(oh[:, k, :, :], over_tiles(first_e[:, :]), over_experts(which[:, k, :]), ALU.is_equal))
                    yield
                    if k == 0:
                        t.wait()
                        t.did(v.scalar_tensor_tensor(out=lg2[:, :, :], in0=oh[:, 0, :, :], scalar=-3.0e38, in1=lg[:, :, :], op0=ALU.mult, op1=ALU.add))
                        yield
                v.tensor_tensor(gap[:, :], best[:, 1, :], best[:, 0, :], ALU.subtract).then_inc(gap_ready, 1)
                t.wait()
                by_tile = chosen[:, :, 1:G + 1].rearrange("p e s -> p s e")
                t.did(v.tensor_tensor(by_tile, oh[:, 0, :, :], oh[:, 1, :, :], ALU.add))
                if not full:
                    t.did(v.tensor_scalar(rowok[:, :], rowok[:, :], float(LAST), None, ALU.is_lt))
                    t.wait()
                    t.did(v.tensor_scalar(chosen[:, :, G], chosen[:, :, G], rowok[:, :], None, ALU.mult))
                yield
                t.wait(apart=dve_passed)
                v.tensor_tensor_scan(out=earlier[:, :, :].rearrange("p e s -> p (e s)"), data0=running[:, :, :].rearrange("p e s -> p (e s)"),
                                     data1=chosen[:, :, :].rearrange("p e s -> p (e s)"), initial=0.0, op0=ALU.mult, op1=ALU.add).then_inc(chosen_ready, 1)
                yield
                t.did(v.tensor_copy(zg[b][:, :, D], tok[:, :]))
                t.did(v.tensor_scalar(zg[b][:, :, D + 1], which[:, 0, :], -1.0, float(E), ALU.mult, ALU.add))
                t.wait()
                t.did(v.tensor_scalar(tok[:, :], tok[:, :], float(G * P), None, ALU.add))
                assert t.n == ROUTE_STEPS or not full, t.n
                yield

            def place(g, b):
                t = Steps(dve, place_step, PLACE_STEPS * g)
                dve.wait_ge(rank_ready, g + 1)
                t.did(v.tensor_tensor(rank[:, :, :], bank[7][:, 0:G * E].rearrange("p (e s) -> p s e", e=E), over_tiles(base_e[:, :]), ALU.add))
                t.did(v.tensor_copy(chosen[:, :, 0], earlier[:, :, G]))
                dve.wait_ge(egap_ready, g + 1)
                t.did(v.tensor_scalar(esum[:, :], egap[:, :], 1.0, None, ALU.add))
                yield
                t.wait()
                t.did(v.reciprocal(wtop[:, :], esum[:, :]))
                t.did(v.tensor_tensor(tmp8b[:, :, :], oh[:, 0, :, :], rank[:, :, :], ALU.mult))
                yield
                t.wait()
                t.did(v.tensor_copy(zg[b][:, :, D + 2], wtop[:, :]))
                t.did(v.tensor_tensor(wsec[:, :], egap[:, :], wtop[:, :], ALU.mult))
                with nc.allow_low_precision(reason="summed in float32, whole numbers below 2^24"):
                    t.did(v.tensor_reduce(pos[b][:, 0, :], tmp8b[:, :, :], AX.X, ALU.add))
                yield
                t.wait()
                t.did(v.tensor_tensor(zg[b][:, :, D + 3], wsec[:, :], wtop[:, :], ALU.subtract))
                t.did(v.tensor_tensor(tmp8b[:, :, :], oh[:, 1, :, :], rank[:, :, :], ALU.mult))
                yield
                t.wait()
                with nc.allow_low_precision(reason="summed in float32, whole numbers below 2^24"):
                    v.tensor_reduce(pos[b][:, 1, :], tmp8b[:, :, :], AX.X, ALU.add).then_inc(routed, 1)
                assert t.n == PLACE_STEPS, t.n

            def group(g, b, first=False, last=False, loads=1):
                t = Steps(dve, stats_step, STATS_STEPS * g)
                scales = iter(()) if last else x_scales(g + 1, 1 - b, loads)
                router = iter(()) if first else route(g - 1, 1 - b)
                places = iter(()) if first or (isinstance(g, int) and g < 2) else place(g - 2, b)

                def fill(steps):
                    next(steps, None)

                if not first:
                    for _ in range(4):
                        fill(scales)
                for _ in places:
                    fill(scales)

                def add(q):
                    lo, hi = PAIRS[q]
                    if not first:
                        for h, part in enumerate(PARTS):
                            if lo == part[0]:
                                dve.wait_ge(x1_out[h], 16 * g)
                        dve.wait_ge(z_ready, G * (g - 1) + hi)
                    dve.wait_ge(g_ready, NP * g + q + 1)
                    v.tensor_tensor(x1g[:, lo:hi, :], bank[2 + q % 2][:, 0:(hi - lo) * D].rearrange("p (s d) -> p s d", d=D),
                                    xg[b][:, lo:hi, :], ALU.add).then_inc(g_added, 1)

                def stats(q):
                    dve.wait_ge(g_added, NP * g + q + 1)
                    for s in range(*PAIRS[q]):
                        t.did(v.bn_stats(bn6[:, 0, s, :], x1g[:, s, :]))
                        for _ in range(6 if q < 2 else 2):
                            fill(scales)
                add(0)
                add(1)
                for q in range(2, NP):
                    stats(q - 2)
                    add(q)
                for q in range(NP - 2, NP):
                    stats(q)
                fill(scales)
                t.wait(apart=dve_passed)
                for s in range(G):
                    t.did(v.bn_aggr(mv[:, 0, s, :], bn6[:, 0, s, :]))
                fill(scales)
                fill(router)
                t.wait()
                t.did(v.tensor_scalar(var_u[:, 0, :], mv[:, 0, :, 1], 1.0 + EPS, EPS * EPS, ALU.mult, ALU.add))
                fill(scales)
                fill(router)
                for _ in rsqrt(t, 0):
                    fill(scales)
                    fill(router)
                t.wait()
                shifts(0, z_scale_ready)
                for _ in scales:
                    pass
                for _ in router:
                    pass
                assert t.n == STATS_STEPS, t.n

            group(0, 0, first=True)
            group(1, 1)
            with dve.Fori(1, GROUPS // 2 - 1) as i:
                for u in range(2):
                    group(2 * i + u, u)
            group(GROUPS - 2, 0, loads=2)
            group(GROUPS - 1, 1, last=True)
            for _ in place(GROUPS - 2, 0):
                pass
            for _ in route(GROUPS - 1, 1, full=False):
                pass
            for _ in place(GROUPS - 1, 1):
                pass

            t = Steps(dve, count_step, 0)
            dve.wait_ge(count_mm, 1)
            t.then(v.tensor_copy(cnt[:, :], bank[6][:, 0:E]))
            t.did(v.tensor_tensor(tail_i[:, :], cnt[0:1, :], base_e[0:1, :], ALU.add))
            t.then(v.tensor_scalar(cnt_i[:, :], cnt[:, :], float(P - 1), None, ALU.add))
            t.then(v.tensor_scalar(tiles_i[:, :], cnt_i[:, :], 7, None, ALU.arith_shift_right))
            t.then(v.tensor_copy(tiles_f[:, :], tiles_i[:, :]))
            t.did(v.tensor_tensor_scan(out=ends[:, :], data0=ones[:, 0:E], data1=tiles_f[:, :], initial=0.0, op0=ALU.mult, op1=ALU.add))
            t.did(v.tensor_scalar(jump[:, :], tiles_f[:, :], float(-P), float(CAP), ALU.mult, ALU.add))
            t.then(v.tensor_scalar(tile_row[:, :], iota_d[:, 0:TABLE], float(P), None, ALU.mult))
            for e in range(E):
                t.did(v.scalar_tensor_tensor(out=tile_e[:, :], in0=iota_d[:, 0:TABLE], scalar=ends[:, e:e + 1], in1=tile_e[:, :], op0=ALU.is_ge, op1=ALU.add))
                t.then(v.tensor_scalar(tmp_t[:, :], iota_d[:, 0:TABLE], ends[:, e:e + 1], jump[:, e:e + 1], ALU.is_ge, ALU.mult))
                t.then(v.tensor_tensor(tile_row[:, :], tile_row[:, :], tmp_t[:, :], ALU.add))
            v.tensor_scalar(tile_i[:, 0, :], tile_e[0:1, :], float(E - 1), None, ALU.min)
            v.tensor_copy(tile_i[:, 1, :], tile_row[0:1, :]).then_inc(tables_ready, 1)

            def meta(i, u):
                j, b = 4 * i + u, u % ZB
                z = zin[b]
                dve.wait_ge(z_in[b], 16 * (i + u // ZB) + 16)
                wait_from(dve, y_out[u % 2], 32 * i + 16 * (u // 2) - 16)
                v.tensor_scalar(second[b][:, :], z[:, D + 1:D + 2], tile_e[:, bass.ds(j, 1)], None, ALU.not_equal).then_inc(meta_step, 1)
                dve.wait_ge(meta_step, j + 1)
                v.tensor_copy(yid[b][:, :], z[:, D:D + 1])
                v.scalar_tensor_tensor(out=ywt[b][:, :], in0=second[b][:, :], scalar=z[:, D + 3:D + 4], in1=z[:, D + 2:D + 3],
                                       op0=ALU.mult, op1=ALU.add).then_inc(meta_ready, 1)

            def x_low(i, u):
                b = u % 2
                dve.wait_ge(xh_ready, 4 * i + u + 1)
                v.tensor_tensor(xl[b][:, :], bank[b][:, 0:D], xh[b][:, :].bitcast(F32), ALU.subtract).then_inc(xl_ready, 1)

            def h_low(i, u):
                j, b = 4 * i + u, u % 2
                dve.wait_ge(hh_ready, j + 1)
                wait_from(dve, y_mm, j)
                v.tensor_tensor(hl[:, :], bank[4 + b][:, :], hh[b][:, :].bitcast(F32), ALU.subtract).then_inc(hl_ready, 1)

            def h_bias(i, u, e):
                j, b = 4 * i + u, u % 2
                wait_from(dve, hT_mm, j - 1)
                dve.wait_ge(h_mm, j + 1)
                v.tensor_tensor(hact[b], bank[2 + b], b1all[:, bass.ds(e, 1), :].rearrange("p a h -> p (a h)"), ALU.add).then_inc(h_added, 1)

            def y_bias(i, u, e):
                j, b = 4 * i + u, u % 2
                wait_from(dve, y_ready[b], 2 * i + u // 2)
                dve.wait_ge(y_mm, j + 1)
                v.tensor_tensor(ysum[b], bank[6 + b][:, 0:D], b2all[:, bass.ds(e, 1), :].rearrange("p a d -> p (a d)"), ALU.add).then_inc(y_added, 1)

            def tile_step(i, u, es, left=4):
                if left > 3:
                    x_low(i, u + 3)
                if left > 2:
                    h_bias(i, u + 2, es[u + 2])
                if left > 1:
                    meta(i, u + 1)
                    h_low(i, u + 1)
                y_bias(i, u, es[u])

            dve.wait_ge(tables_ready, 1)
            es = experts(nc, dve, tile_i[:, 0, :], 0)
            x_low(0, 0)
            x_low(0, 1)
            dve.wait_ge(b1_in, 16)
            h_bias(0, 0, es[0])
            x_low(0, 2)
            h_bias(0, 1, es[1])
            meta(0, 0)
            h_low(0, 0)
            dve.wait_ge(b2_in, 16)
            for u in range(4):
                tile_step(0, u, es)
            with dve.Fori(1, NT // 4 - 1) as i:
                es = experts(nc, dve, tile_i[:, 0, :], i)
                for u in range(4):
                    tile_step(i, u, es)
            es = experts(nc, dve, tile_i[:, 0, :], NT // 4 - 1)
            for u in range(4):
                tile_step(NT // 4 - 1, u, es, 4 - u)

        @block.scalar
        def _(act):
            def copy(out_, in_):
                return nc.scalar.activation(out_, in_, ACT.Copy)
            act.wait_ge(s_const, 4)
            act.wait_ge(score_zeroed, 1)
            tv = score.rearrange("p (b r) -> p b r", b=EBLK)
            for q in range(4):
                hi = min(4 * q + 4, EBLK)
                act.wait_ge(block_turned, hi)
                full = hi - 4 * q - (1 if q == 3 else 0)
                bv = bank[q].rearrange("p (b r) -> p b r", b=4)
                ins = copy(tv[:, 4 * q:4 * q + full, :], bv[:, 0:full, 0:EROWS])
                if q == 3:
                    ins = copy(tv[0:ELAST, EBLK - 1, :], bv[0:ELAST, full, 0:EROWS])
                ins.then_inc(block_out, 1)
            act.wait_ge(small_in, 80)
            def high1(i, b):
                e, k = 2 * i + b // 2, b % 2
                act.wait_ge(stage_in[b], 16 * i + 16)
                nc.scalar.activation(w1h[:, bass.ds(e, 1), k, :].rearrange("p a h -> p (a h)"), stage[b], ACT.Copy,
                                     scale=gam[:, k:k + 1]).then_inc(w_high, 1)
                wait_from(act, w_low, SB * i + b - 1)
                nc.scalar.activation(scaled[k], stage[b], ACT.Copy, scale=gam[:, k:k + 1]).then_inc(w_product, 1)
            for b in range(SB):
                high1(0, b)
            with act.Fori(1, E // 2) as i:
                for b in range(SB):
                    high1(i, b)
            def high2(lo, hi):
                with act.Fori(lo, hi) as i:
                    for b in range(SB):
                        e, k = 2 * i + b // 2, b % 2
                        act.wait_ge(stage_in[b], 16 * i + 16 * (PIECES // SB) + 16)
                        copy(w2h[:, bass.ds(e, 1), 2 * k:2 * k + 2, :].rearrange("p a k d -> p (a k d)"), stage[b]).then_inc(w_high, 1)
            high2(0, HALF)

            def x_norm(g, s, b):
                wait_from(act, xT_mm, NP * (g - 1) + s // 2 + 1)
                nc.scalar.activation(xn[:, s, :], xg[b][:, s, :], ACT.Identity, scale=rs[:, 1, s:s + 1],
                                     bias=shift[:, 1, s:s + 1]).then_inc(xn_ready, 1)

            def z_norm(g, s, b):
                nc.scalar.activation(zg[b][:, s, 0:D], x1g[:, s, :], ACT.Identity, scale=rs[:, 0, s:s + 1],
                                     bias=shift[:, 0, s:s + 1]).then_inc(z_ready, 1)

            def width(q):
                return (PAIRS[q][1] - PAIRS[q][0]) * D

            def x_copy(g, q):
                act.wait_ge(xT_mm, NP * g + q + 1)
                wait_from(act, g_ready, used(g, q))
                copy(xT[q % 2][:, 0:width(q)], bank[q % 2][:, 0:width(q)]).then_inc(xT_ready, 1)

            def z_copy(g, q):
                act.wait_ge(zT_mm, NP * g + q + 1)
                wait_from(act, logits_ready, used(g, q))
                copy(zT[q % 2][:, 0:width(q)], bank[4 + q % 2][:, 0:width(q)]).then_inc(zT_ready, 1)

            def exp_gap(g):
                act.wait_ge(gap_ready, g + 1)
                nc.scalar.activation(egap[:, :], gap[:, :], ACT.Exp).then_inc(egap_ready, 1)

            def group(g, b, x_side=True, z_side=True, older=True):
                if x_side:
                    act.wait_ge(x_scale_ready, g + 1)
                    for s in range(3):
                        x_norm(g, s, b)
                    x_copy(g, 0)
                    x_norm(g, 3, b)
                    x_norm(g, 4, b)
                    x_copy(g, 1)
                    x_norm(g, 5, b)
                    x_norm(g, 6, b)
                    x_copy(g, 2)
                if older:
                    exp_gap(g - 2)
                if z_side:
                    act.wait_ge(z_scale_ready, g)
                    wait_from(act, sent[1 - b], 16 * G * (g - 1 - (1 - b)))
                    for s in range(4):
                        z_norm(g - 1, s, 1 - b)
                    z_copy(g - 1, 0)
                if x_side:
                    x_copy(g, 3)
                if z_side:
                    z_norm(g - 1, 4, 1 - b)
                    z_norm(g - 1, 5, 1 - b)
                    z_copy(g - 1, 1)
                    z_norm(g - 1, 6, 1 - b)
                    z_copy(g - 1, 2)
                    z_copy(g - 1, 3)

            act.wait_ge(table_ready, 1)
            act.wait_ge(w_low, PIECES)
            group(0, 0, z_side=False, older=False)
            high2(HALF, E // 2)
            act.wait_ge(w_low, 2 * PIECES)
            group(1, 1, older=False)
            group(2, 0)
            group(3, 1)
            with act.Fori(2, GROUPS // 2) as i:
                for u in range(2):
                    group(2 * i + u, u)
            group(GROUPS, 0, x_side=False)
            exp_gap(GROUPS - 1)
            nc.scalar.activation(first_gelu[:, :], ident[:, 0:1], ACT.Gelu)

            def x_high(i, u):
                j, b = 4 * i + u, u % 2
                act.wait_ge(zx_mm, j + 1)
                wait_from(act, h_mm, j - 1)
                copy(xh[b][:, :], bank[b][:, 0:D]).then_inc(xh_ready, 1)

            def gelu(i, u):
                j, b = 4 * i + u, u % 2
                act.wait_ge(h_added, j + 1)
                nc.scalar.activation(hact[b], hact[b], ACT.Gelu).then_inc(h_ready, 1)

            def h_high(i, u):
                j, b = 4 * i + u, u % 2
                act.wait_ge(hT_mm, j + 1)
                wait_from(act, y_mm, j - 1)
                copy(hh[b][:, :], bank[4 + b][:, :]).then_inc(hh_ready, 1)

            def y_scale(i, u):
                j, b = 4 * i + u, u % 2
                act.wait_ge(y_added, j + 1)
                act.wait_ge(meta_ready, j + 1)
                wait_from(act, y_out[b], 32 * i + 16 * (u // 2))
                nc.scalar.activation(ysb[b][:, :], ysum[b], ACT.Copy, scale=ywt[u % ZB][:, :]).then_inc(y_ready[b], 1)

            def tile_step(i, u, left=4):
                if left > 3:
                    x_high(i, u + 3)
                if not (isinstance(i, int) and i == 0 and u == 0):
                    y_scale(i, u - 1)
                if left > 1:
                    h_high(i, u + 1)
                if left > 2:
                    gelu(i, u + 2)

            x_high(0, 0)
            x_high(0, 1)
            gelu(0, 0)
            x_high(0, 2)
            gelu(0, 1)
            h_high(0, 0)
            for u in range(4):
                tile_step(0, u)
            with act.Fori(1, NT // 4 - 1) as i:
                for u in range(4):
                    tile_step(i, u)
            for u in range(4):
                tile_step(NT // 4 - 1, u, 4 - u)
            y_scale(NT // 4 - 1, 3)


_INS = ['x', 'src', 'dst', 'edge_weight', 'L0_ffn_gamma', 'L0_ffn_beta', 'L0_ffn_Wr', 'L0_ffn_br', 'L0_ffn_W1', 'L0_ffn_b1',
        'L0_ffn_W2', 'L0_ffn_b2']


def kernel(**inputs):
    import concourse.bacc as bacc
    from concourse.bass_utils import run_bass_kernel_spmd
    nc = bacc.Bacc("TRN2", target_bir_lowering=False, num_devices=1)
    arrays, args = {}, []
    for name in _INS:
        a = np.ascontiguousarray(inputs[name])
        arrays[f"in_{name}_dram"] = a
        args.append(nc.dram_tensor(f"in_{name}_dram", a.shape, mybir.dt.from_np(a.dtype), kind="ExternalInput").ap())
    args.append(nc.dram_tensor("out_0_dram", (OUT_ROWS, D), F32, kind="ExternalOutput").ap())
    build(nc, *args)
    r = run_bass_kernel_spmd(nc, [arrays], core_ids=[0])
    return r.results[0]["out_0_dram"][0:N]
```
